# Optimizing a Trainium2 kernel written in Bass

```python
import numpy as np
import jax
import jax.numpy as jnp

def _softmax(x, axis=-1):
    return jax.nn.softmax(x, axis=axis)

def _gelu(x):
    return jax.nn.gelu(x, approximate=True)

def _silu(x):
    return jax.nn.silu(x)

def _sigmoid(x):
    return jax.nn.sigmoid(x)

def _layernorm(x, axis=-1, eps=1e-05):
    m = jnp.mean(x, axis=axis, keepdims=True)
    v = jnp.var(x, axis=axis, keepdims=True)
    return (x - m) / jnp.sqrt(v + eps)

def _scatter_add(tgt, idx, src, axis=0):
    return tgt.at[idx].add(src)

def _segment_sum(src, seg, n):
    return jax.ops.segment_sum(src, seg, n)
kernel_name = 'mk_xattn_seq_d2_seqx_r2_52002c'

def setup_inputs(seed: int=0):
    np.random.seed(seed)
    _w = jnp.asarray

    def _rec_inputs():
        import jax
        import jax.numpy as jnp
        _rk = jax.random.key(seed)
        x = -0.0005207 + 1.001 * jax.random.normal(jax.random.fold_in(_rk, 1), (2, 2048, 512), jnp.float32)
        _lenS = 2048 - jax.random.randint(jax.random.fold_in(_rk, 7), (2,), 0, max(1, 2048 // 4) + 1, jnp.int32)
        _lenS2 = 77 - jax.random.randint(jax.random.fold_in(_rk, 8), (2,), 0, max(1, 77 // 4) + 1, jnp.int32)
        _ctx_1024P = jax.random.normal(jax.random.fold_in(_rk, 11), (2, 16, 512), jnp.float32)
        _ctx_1024c = jax.random.dirichlet(jax.random.fold_in(_rk, 511), 0.3 * jnp.ones((16,), jnp.float32), (2, 77))
        _ctx_1024t = jnp.einsum('bsk,bkd->bsd', _ctx_1024c, _ctx_1024P)
        _ctx_1024t = _ctx_1024t * jax.lax.rsqrt(jnp.mean(jnp.square(_ctx_1024t)) + 1e-12) * 0.953939
        ctx_1024 = 4.13588e-05 + 0.999923 * (_ctx_1024t + 0.3 * jax.random.normal(jax.random.fold_in(_rk, 611), (2, 77, 512), jnp.float32))
        itok_S_0_4092 = jax.random.randint(jax.random.fold_in(_rk, 12), (2048,), 0, 4093, jnp.int32)
        return (x, ctx_1024, itok_S_0_4092)
    x, ctx_1024, itok_S_0_4092 = _rec_inputs()

    def _L0_xattn_setup():
        import jax, jax.numpy as jnp
        import numpy as np
        B, Q, K, D, H = (2, 512, 2048, 512, 16)
        DH = D // H
        LN_EPS = 1e-05

        def char_aware_mask(wb, cb, q_len, k_len):
            ws, we = (wb[:-1], wb[1:])
            nW = ws.shape[0]
            cs = cb[ws]
            ce = cb[we - 1]
            q = jnp.arange(q_len)
            i = jnp.clip(jnp.searchsorted(wb, q, side='right') - 1, 0, nW - 1)
            valid = (q >= ws[i]) & (q < we[i])
            j = jnp.arange(k_len)[None, :]
            in_char = (j >= cs[i][:, None]) & (j < ce[i][:, None])
            ps = ws[jnp.maximum(i - 1, 0)]
            in_prev = (i > 0)[:, None] & (j >= ps[:, None]) & (j < ws[i][:, None])
            ns = we[i]
            ne = wb[jnp.minimum(i + 2, nW)]
            in_next = (i < nW - 1)[:, None] & (j >= ns[:, None]) & (j < ne[:, None])
            return (valid[:, None] & (in_char | in_prev | in_next)).astype(jnp.float32)
        key = jax.random.key(seed)
        ks = jax.random.split(key, 10)
        queries = jax.random.normal(ks[0], (B, Q, D), jnp.float32)
        keys = jax.random.normal(ks[1], (B, K, D), jnp.float32)
        values = jax.random.normal(ks[2], (B, K, D), jnp.float32)
        word_boundaries = jnp.arange(0, Q + 1, 8, dtype=jnp.int32)
        char_boundaries = jnp.sort(jax.random.randint(ks[3], (Q,), 0, K + 1, dtype=jnp.int32))
        s = 0.02
        ln_gamma = jnp.ones((D,), jnp.float32)
        ln_beta = jnp.zeros((D,), jnp.float32)
        in_proj_w = jax.random.normal(ks[4], (3 * D, D), jnp.float32) * s
        in_proj_b = jnp.zeros((3 * D,), jnp.float32)
        out_w = jax.random.normal(ks[5], (D, D), jnp.float32) * s
        out_b = jnp.zeros((D,), jnp.float32)
        return dict(queries=queries, keys=keys, values=values, word_boundaries=word_boundaries, char_boundaries=char_boundaries, ln_gamma=ln_gamma, ln_beta=ln_beta, in_proj_w=in_proj_w, in_proj_b=in_proj_b, out_w=out_w, out_b=out_b)
    _L0_xattn_all = _L0_xattn_setup()
    _L0_xattn_in = {k: v for k, v in _L0_xattn_all.items() if k in ('word_boundaries', 'ln_gamma', 'ln_beta', 'in_proj_w', 'in_proj_b', 'out_w', 'out_b')}
    del _L0_xattn_all

    def _L1_xattn_setup():
        import jax, jax.numpy as jnp
        import numpy as np
        MODEL_DIM = 512
        NUM_HEADS = 8
        B, L = (16, 1024)
        key = jax.random.key(seed)
        ks = jax.random.split(key, 12)
        s = 1.0 / np.sqrt(MODEL_DIM)
        d = MODEL_DIM
        return {'query': jax.random.normal(ks[0], (B, L, d), jnp.float32), 'key_': jax.random.normal(ks[1], (B, L, d), jnp.float32), 'value': jax.random.normal(ks[2], (B, L, d), jnp.float32), 'Wq': jax.random.uniform(ks[3], (d, d), jnp.float32, -s, s), 'bq': jax.random.uniform(ks[4], (d,), jnp.float32, -s, s), 'Wk': jax.random.uniform(ks[5], (d, d), jnp.float32, -s, s), 'bk': jax.random.uniform(ks[6], (d,), jnp.float32, -s, s), 'Wv': jax.random.uniform(ks[7], (d, d), jnp.float32, -s, s), 'bv': jax.random.uniform(ks[8], (d,), jnp.float32, -s, s), 'Wo': jax.random.uniform(ks[9], (d, d), jnp.float32, -s, s), 'bo': jax.random.uniform(ks[10], (d,), jnp.float32, -s, s)}
    _L1_xattn_all = _L1_xattn_setup()
    _L1_xattn_in = {k: v for k, v in _L1_xattn_all.items() if k in ('Wq', 'bq', 'Wk', 'bk', 'Wv', 'bv', 'Wo', 'bo')}
    del _L1_xattn_all
    return {'x': x, 'ctx_1024': ctx_1024, 'itok_S_0_4092': itok_S_0_4092, 'L0_xattn_word_boundaries': _L0_xattn_in['word_boundaries'], 'L0_xattn_ln_gamma': _L0_xattn_in['ln_gamma'], 'L0_xattn_ln_beta': _L0_xattn_in['ln_beta'], 'L0_xattn_in_proj_w': _L0_xattn_in['in_proj_w'], 'L0_xattn_in_proj_b': _L0_xattn_in['in_proj_b'], 'L0_xattn_out_w': _L0_xattn_in['out_w'], 'L0_xattn_out_b': _L0_xattn_in['out_b'], 'L1_xattn_Wq': _L1_xattn_in['Wq'], 'L1_xattn_bq': _L1_xattn_in['bq'], 'L1_xattn_Wk': _L1_xattn_in['Wk'], 'L1_xattn_bk': _L1_xattn_in['bk'], 'L1_xattn_Wv': _L1_xattn_in['Wv'], 'L1_xattn_bv': _L1_xattn_in['bv'], 'L1_xattn_Wo': _L1_xattn_in['Wo'], 'L1_xattn_bo': _L1_xattn_in['bo']}

def reference(x, ctx_1024, itok_S_0_4092, L0_xattn_word_boundaries, L0_xattn_ln_gamma, L0_xattn_ln_beta, L0_xattn_in_proj_w, L0_xattn_in_proj_b, L0_xattn_out_w, L0_xattn_out_b, L1_xattn_Wq, L1_xattn_bq, L1_xattn_Wk, L1_xattn_bk, L1_xattn_Wv, L1_xattn_bv, L1_xattn_Wo, L1_xattn_bo):
    import jax
    import jax.numpy as jnp

    def _L0_xattn_ref(queries, keys, values, word_boundaries, char_boundaries, ln_gamma, ln_beta, in_proj_w, in_proj_b, out_w, out_b):
        import jax, jax.numpy as jnp
        import numpy as np
        B, Q, K, D, H = (2, 512, 2048, 512, 16)
        DH = D // H
        LN_EPS = 1e-05

        def char_aware_mask(wb, cb, q_len, k_len):
            ws, we = (wb[:-1], wb[1:])
            nW = ws.shape[0]
            cs = cb[ws]
            ce = cb[we - 1]
            q = jnp.arange(q_len)
            i = jnp.clip(jnp.searchsorted(wb, q, side='right') - 1, 0, nW - 1)
            valid = (q >= ws[i]) & (q < we[i])
            j = jnp.arange(k_len)[None, :]
            in_char = (j >= cs[i][:, None]) & (j < ce[i][:, None])
            ps = ws[jnp.maximum(i - 1, 0)]
            in_prev = (i > 0)[:, None] & (j >= ps[:, None]) & (j < ws[i][:, None])
            ns = we[i]
            ne = wb[jnp.minimum(i + 2, nW)]
            in_next = (i < nW - 1)[:, None] & (j >= ns[:, None]) & (j < ne[:, None])
            return (valid[:, None] & (in_char | in_prev | in_next)).astype(jnp.float32)
        b, q_len, d = queries.shape
        k_len = keys.shape[1]
        mask = char_aware_mask(word_boundaries, char_boundaries, q_len, k_len)
        mu = jnp.mean(queries, axis=-1, keepdims=True)
        var = jnp.var(queries, axis=-1, keepdims=True)
        x = (queries - mu) * jax.lax.rsqrt(var + LN_EPS) * ln_gamma + ln_beta
        wq, wk, wv = jnp.split(in_proj_w, 3, axis=0)
        bq, bk, bv = jnp.split(in_proj_b, 3)
        qh = (x @ wq.T + bq).reshape(b, q_len, H, DH)
        kh = (keys @ wk.T + bk).reshape(b, k_len, H, DH)
        vh = (values @ wv.T + bv).reshape(b, k_len, H, DH)
        scale = 1.0 / jnp.sqrt(jnp.asarray(DH, queries.dtype))
        scores = jnp.einsum('bqhd,bkhd->bhqk', qh * scale, kh) + mask[None, None]
        attn = jax.nn.softmax(scores, axis=-1)
        ctx = jnp.einsum('bhqk,bkhd->bqhd', attn, vh).reshape(b, q_len, d)
        out = ctx @ out_w.T + out_b
        return queries + out

    def _L1_xattn_ref(query, key_, value, Wq, bq, Wk, bk, Wv, bv, Wo, bo):
        import jax, jax.numpy as jnp
        import numpy as np
        MODEL_DIM = 512
        NUM_HEADS = 8
        B, L = (16, 1024)
        residual = query
        q = jnp.einsum('bld,de->ble', query, Wq) + bq
        k = jnp.einsum('bld,de->ble', key_, Wk) + bk
        v = jnp.einsum('bld,de->ble', value, Wv) + bv
        scale = (MODEL_DIM // NUM_HEADS) ** (-0.5)
        attn = jnp.einsum('bqd,bkd->bqk', q, k) * scale
        attn = jax.nn.softmax(attn, axis=-1)
        ctx = jnp.einsum('bqk,bkd->bqd', attn, v)
        out = jnp.einsum('bld,de->ble', ctx, Wo) + bo
        return residual + out
    x = _L0_xattn_ref(x, ctx_1024, ctx_1024, L0_xattn_word_boundaries, itok_S_0_4092, L0_xattn_ln_gamma, L0_xattn_ln_beta, L0_xattn_in_proj_w, L0_xattn_in_proj_b, L0_xattn_out_w, L0_xattn_out_b)
    x = _L1_xattn_ref(x, ctx_1024, ctx_1024, L1_xattn_Wq, L1_xattn_bq, L1_xattn_Wk, L1_xattn_bk, L1_xattn_Wv, L1_xattn_bv, L1_xattn_Wo, L1_xattn_bo)
    return x

_drawn_inputs = setup_inputs


def setup_inputs(seed=0):
    import zlib

    import numpy as np

    out = dict(_drawn_inputs(seed))
    spreads = {'L0_xattn_ln_gamma': (1.0, 0.6),
     'L0_xattn_ln_beta': (0.0, 0.8),
     'L0_xattn_in_proj_b': (0.0, 0.1),
     'L0_xattn_out_b': (0.0, 0.1)}
    factors = {'L1_xattn_bq': 8.0, 'L1_xattn_bk': 8.0, 'L1_xattn_bv': 4.008}
    for name, (base, spread) in spreads.items():
        noise = np.random.default_rng([zlib.crc32(name.encode()), seed]).standard_normal(out[name].shape)
        drawn = base * np.exp(spread * noise) if base else spread * noise
        out[name] = jnp.asarray(drawn.astype(out[name].dtype))
    for name, factor in factors.items():
        out[name] = (out[name] * factor).astype(out[name].dtype)
    return out
```

```python
from contextlib import ExitStack

import concourse.bass as bass
from concourse import mybir

ALU = mybir.AluOpType
ACT = mybir.ActivationFunctionType
AX = mybir.AxisListType
F32 = mybir.dt.float32
F32R = mybir.dt.float32r
BF16 = mybir.dt.bfloat16
I32 = mybir.dt.int32

P = 128
EPS = 1e-5


def two_cross_attentions(
    nc: bass.Bass,
    x: bass.AP,
    ctx_in: bass.AP,
    char_bounds: bass.AP,
    word_bounds: bass.AP,
    gamma: bass.AP,
    beta: bass.AP,
    w_in: bass.AP,
    b_in: bass.AP,
    w_out: bass.AP,
    b_out: bass.AP,
    wq1: bass.AP,
    bq1: bass.AP,
    wk1: bass.AP,
    bk1: bass.AP,
    wv1: bass.AP,
    bv1: bass.AP,
    wo1: bass.AP,
    bo1: bass.AP,
    out: bass.AP,
):
    B, S, D = x.shape
    J = ctx_in.shape[1]
    H = 16
    DH = D // H
    KT = D // P
    HPT = P // DH
    W = word_bounds.shape[0] - 1
    T = 512
    SUB = T // P
    QT = S // T
    NT = B * QT
    NCB = char_bounds.shape[0]
    CC = NCB // P
    SCALE0 = float(DH) ** -0.5
    SCALE1 = float(D // 8) ** -0.5
    GJ = HPT * J
    BJ = B * J
    NV = 8
    assert B == 2 and D == 512 and J <= 77 and W == 64 and CC == 16 and DH == 32

    x_t = x.rearrange("b (q s p) d -> b q p s d", s=SUB, p=P)
    out_t = out.rearrange("b (q s p) d -> b q p s d", s=SUB, p=P)

    with ExitStack() as ctx:
        def sem(name):
            return ctx.enter_context(nc.semaphore(name))

        def keep(name, shape, dt):
            return ctx.enter_context(nc.sbuf_tensor(name, shape, dt))

        wqT_hi = keep("wqT_hi", [P, KT, D], F32R)
        wqT_lo = keep("wqT_lo", [P, KT, D], F32R)
        woT_hi = keep("woT_hi", [P, KT, D], F32R)
        woT_lo = keep("woT_lo", [P, KT, D], F32R)
        kdiag_hi = keep("kdiag_hi", [P, B, KT, GJ], F32R)
        kdiag_lo = keep("kdiag_lo", [P, B, KT, GJ], F32R)
        kstack = keep("kstack", [96, B, H, J], F32R)
        auxw = keep("auxw", [96, H, J], F32R)
        v0 = keep("v0", [J, B, D], F32)
        vw1 = keep("vw1", [J + 2, B, D], F32)
        m_hi = keep("m_hi", [P, KT, B, J], F32R)
        m_lo = keep("m_lo", [P, KT, B, J], F32R)
        w2_hi = keep("w2_hi", [P, KT, B, J], F32R)
        w2_lo = keep("w2_lo", [P, KT, B, J], F32R)
        colm = keep("colm", [P, B, J], F32)
        cvec = keep("cvec", [P, B, J], F32)
        ident = keep("ident", [P, P], F32)
        ones = keep("ones", [P, P], F32)
        q_bias = keep("q_bias", [P, KT], F32)
        tok = keep("tok", [W, T], F32)
        wlo = keep("wlo", [W, 1], F32)
        whi = keep("whi", [W, 1], F32)
        vcols = keep("vcols", [P, NV * KT], F32)

        bank = [ctx.enter_context(nc.psum_tensor(f"bank{i}", [P, 512], F32)) for i in range(8)]

        with ExitStack() as prep:
            def tmp(name, shape, dt):
                return prep.enter_context(nc.sbuf_tensor(name, shape, dt))

            w_in_sb = tmp("w_in_sb", [P, 3 * KT, D], F32)
            w_out_sb = tmp("w_out_sb", [P, KT, D], F32)
            wq1_sb = tmp("wq1_sb", [P, KT, D], F32)
            wk1_sb = tmp("wk1_sb", [P, KT, D], F32)
            wv1_sb = tmp("wv1_sb", [P, KT, D], F32)
            wo1_sb = w_in_sb[:, 0:KT, :]
            ctx_sb = tmp("ctx_sb", [J, B, D], F32)
            ctxT0 = tmp("ctxT0", [P, KT, BJ], F32)
            wT = tmp("wT", [P, 2, KT, D], F32)
            kT = tmp("kT", [P, KT, B, J], F32)
            kT_hi = tmp("kT_hi", [P, KT, B, J], F32R)
            kT_lo = tmp("kT_lo", [P, KT, B, J], F32R)
            k1T = tmp("k1T", [P, KT, BJ], F32)
            v1T = tmp("v1T", [P, KT, BJ], F32)
            m_f = tmp("m_f", [P, KT, B, J], F32)
            w2_f = tmp("w2_f", [P, KT, B, J], F32)
            vrows = tmp("vrows", [NV * KT, P], F32)
            rep = tmp("rep", [P, 2, KT, P], F32)
            bv_row = tmp("bv_row", [1, D], F32)
            gs = tmp("gs", [P, KT], F32)
            cb_i = tmp("cb_i", [CC, P], I32)
            cb_f = tmp("cb_f", [CC, P], F32)
            cb_c = tmp("cb_c", [P, CC], BF16)
            wb_i = tmp("wb_i", [P, W + 1], I32)
            widx = tmp("widx", [P, 2 * W], F32)
            widx2 = tmp("widx2", [P, 2 * W], F32)
            kcol = tmp("kcol", [P, CC], F32)
            pick = tmp("pick", [P, CC, 2 * W], BF16)
            wcol_i = tmp("wcol_i", [W, 4], I32)
            wcol = tmp("wcol", [W, 4], F32)
            ce_cs = tmp("ce_cs", [P, 1], F32)
            ce_cs2 = tmp("ce_cs2", [P, 1], F32)
            p1ones = tmp("p1ones", [P, 2], F32)
            dve_mark = tmp("dve_mark", [P, 1], F32)
            cend = tmp("cend", [W, 1], F32)
            ge = tmp("ge", [W, 3, J], F32)
            rng = tmp("rng", [W, 3, J], F32)
            aux_f = tmp("aux_f", [P, H, J], F32)
            wb32 = tmp("wb32", [P, W + 1], F32)

        xs = [keep(f"x{i}", [P, SUB, D], F32) for i in range(2)]
        z = keep("z", [P, 2, D], F32)
        zT_hi = keep("zT_hi", [P, KT, T], F32R)
        zT_lo = keep("zT_lo", [P, KT, T], F32R)
        q_hi = keep("q_hi", [P, KT, T], F32R)
        q_lo = keep("q_lo", [P, KT, T], F32R)
        qstack = keep("qstack", [96, H, T], F32R)
        auxq = keep("auxq", [96, T], F32R)
        prob = keep("prob", [J, 2, T], F32)
        att = keep("att", [P, 2, T], F32)
        attT_hi = keep("attT_hi", [P, KT, T], F32R)
        attT_lo = keep("attT_lo", [P, KT, T], F32R)
        s1z = keep("s1z", [J, 2, T], F32)
        s1t = keep("s1t", [J + 2, T], F32)
        stats = keep("stats", [P, SUB, 6], F32)
        mean = [keep(f"mean{i}", [P, SUB], F32) for i in range(2)]
        mdiff = keep("mdiff", [P, SUB], F32)
        veps = keep("veps", [P, SUB], F32)
        mhalf = keep("mhalf", [P, SUB], F32)
        rstd = keep("rstd", [P, SUB], F32)
        std = [keep(f"std{i}", [P, SUB], F32) for i in range(2)]
        mx = keep("mx", [P, SUB, H], F32)
        mx_hr = keep("mx_hr", [P, SUB, H], F32R)
        mx2 = keep("mx2", [P, SUB, 2 * H], F32)
        p1 = keep("p1", [P, SUB, J + 2], F32)
        sc1 = p1[:, :, 0:J]
        sc1b = keep("sc1b", [P, SUB, J], F32)
        nmax1 = keep("nmax1", [P, SUB], F32)
        sum1 = keep("sum1", [P, SUB], F32)
        rsum1 = keep("rsum1", [P, SUB], F32)
        e1 = sc1b

        s_vec = sem("s_vec")
        s_word = sem("s_word")
        s_ctx = sem("s_ctx")
        s_wq = sem("s_wq")
        s_wkv = sem("s_wkv")
        s_w1 = sem("s_w1")
        s_bias1 = sem("s_bias1")
        s_kstack = sem("s_kstack")
        const_ready = sem("const_ready")
        job_done = sem("job_done")
        act_took = sem("act_took")
        dve_took = sem("dve_took")
        pool_step = sem("pool_step")
        cb_ready = sem("cb_ready")
        gs_ready = sem("gs_ready")
        hi_done = sem("hi_done")
        wo_split = sem("wo_split")
        prep_lo = sem("prep_lo")
        wq_split = sem("wq_split")
        k_split = sem("k_split")
        prep_step = sem("prep_step")
        rep_ready = sem("rep_ready")
        pick_ready = sem("pick_ready")
        act_prepared = sem("act_prepared")
        dve_prepared = sem("dve_prepared")
        x_loaded = [sem(f"x_loaded{i}") for i in range(2)]
        x_stored = sem("x_stored")
        stack_loaded = sem("stack_loaded")
        step = sem("step")
        veps_ready = sem("veps_ready")
        rstd_ready = sem("rstd_ready")
        mhalf_ready = sem("mhalf_ready")
        z_ready = sem("z_ready")
        z_turned = sem("z_turned")
        zhi_ready = sem("zhi_ready")
        zlo_ready = sem("zlo_ready")
        q_done = sem("q_done")
        qhi_ready = sem("qhi_ready")
        qlo_ready = sem("qlo_ready")
        s1z_done = sem("s1z_done")
        s1z_ready = sem("s1z_ready")
        maxs_done = sem("maxs_done")
        max_taken = sem("max_taken")
        mx_ready = sem("mx_ready")
        mx_turned = sem("mx_turned")
        auxq_ready = sem("auxq_ready")
        onehot_ready = sem("onehot_ready")
        scores_done = sem("scores_done")
        prob_ready = sem("prob_ready")
        head_used = sem("head_used")
        att_ready = sem("att_ready")
        atthi_ready = sem("atthi_ready")
        attlo_ready = sem("attlo_ready")
        s1a_done = sem("s1a_done")
        s1a_ready = sem("s1a_ready")
        s1_turned = sem("s1_turned")
        nmax1_ready = sem("nmax1_ready")
        e1_ready = sem("e1_ready")
        p1_ready = sem("p1_ready")
        p1_turned = sem("p1_turned")
        p1T_ready = sem("p1T_ready")
        out_done = sem("out_done")
        out_ready = sem("out_ready")

        def at(t, per, c):
            return t * per + c

        JV = 0
        JCTX = 1
        JWQ = 3
        JWK = JWQ + KT
        JQB = JWK + KT
        JK = JQB + 1
        JWV = JK + KT
        JVV = JWV + KT
        JWO = JVV + B
        JWQ1 = JWO + KT
        JK1 = JWQ1 + KT
        JV1 = JK1 + KT
        JM = JV1 + KT
        JW2 = JM + KT
        JCOL = JW2 + KT
        JC = JCOL + 1
        JVW = JC + 1
        JP = JVW + B
        NJ = JP + 1
        TURN_AT = (7, 9, 11, 13)
        V_BQ, V_BK, V_GAMMA, V_BETA, V_BOUT, V_BQ1, V_BK1, V_BV1 = range(NV)

        def taken(eng, n):
            if n % 2 == 0:
                eng.wait_ge(act_took, n // 2 + 1)
            else:
                eng.wait_ge(dve_took, n // 2 + 1)

        def vcol(v, k):
            return vcols[:, v * KT + k:v * KT + k + 1]

        block = ctx.enter_context(nc.Block())

        @block.sync
        def _(sp):
            vecs = [b_in[0:D], b_in[D:2 * D], gamma, beta, b_out, bq1, bk1, bv1]
            for n, v in enumerate(vecs):
                sp.dma_start(vrows[n * KT:(n + 1) * KT, :], v.rearrange("(k p) -> k p", p=P)).then_inc(s_vec, 16)
            sp.dma_start(cb_i[:, :], char_bounds.rearrange("(c p) -> c p", p=P)).then_inc(s_vec, 16)
            sp.dma_start(ctx_sb[:, :, :], ctx_in.rearrange("b j d -> j b d")).then_inc(s_ctx, 16)
            w_in_v = w_in.rearrange("(t p) d -> p t d", p=P)
            sp.dma_start(w_in_sb[:, 0:KT, :], w_in_v[:, 0:KT, :]).then_inc(s_wq, 16)
            wb = word_bounds.rearrange("(w o) -> w o", o=1)
            with nc.allow_non_contiguous_dma(reason="65 word boundaries, one per partition"):
                for dst, src in (((0, W, 0), (0, W)), ((0, W, 1), (1, W + 1)),
                                 ((0, 1, 2), (0, 1)), ((1, W, 2), (0, W - 1)),
                                 ((0, W - 1, 3), (2, W + 1)), ((W - 1, W, 3), (W, W + 1))):
                    sp.dma_start(wcol_i[dst[0]:dst[1], dst[2]:dst[2] + 1], wb[src[0]:src[1], :]).then_inc(s_word, 16)
            sp.dma_start(wb_i[:, :], word_bounds.rearrange("(o w) -> o w", o=1).broadcast_to([P, W + 1])).then_inc(s_word, 16)
            sp.dma_start(bv_row[:, :], b_in[2 * D:3 * D].rearrange("(o d) -> o d", o=1)).then_inc(s_vec, 16)
            sp.dma_start(w_in_sb[:, KT:3 * KT, :], w_in_v[:, KT:3 * KT, :]).then_inc(s_wkv, 16)
            for dst, src in ((w_out_sb, w_out), (wq1_sb, wq1), (wk1_sb, wk1), (wv1_sb, wv1), (wo1_sb, wo1)):
                if dst is wo1_sb:
                    sp.wait_ge(job_done, JWQ + KT)
                sp.dma_start(dst[:, :, :], src.rearrange("(t p) d -> p t d", p=P)).then_inc(s_w1, 16)
            for b in range(B):
                sp.dma_start(vw1[J:J + 1, b, :], bo1.rearrange("(o d) -> o d", o=1)).then_inc(s_bias1, 16)
                sp.dma_start(vw1[J + 1:J + 2, b, :], b_out.rearrange("(o d) -> o d", o=1)).then_inc(s_bias1, 16)
            sp.wait_ge(k_split, 1)
            for slot, src in enumerate((kT_hi, kT_hi, kT_lo)):
                for a in range(HPT):
                    for b in range(B):
                        sp.dma_start(kstack[DH * slot:DH * (slot + 1), b, a::HPT, :].bitcast(F32),
                                     src[DH * a:DH * (a + 1), :, b, :].bitcast(F32)).then_inc(s_kstack, 16)
            sp.wait_ge(s_kstack, 16 * 3 * HPT * B)
            sp.wait_ge(job_done, NJ)
            sp.wait_ge(act_prepared, 1)
            sp.wait_ge(dve_prepared, 1)

            def load(t, q, s):
                if t is not None:
                    sp.wait_ge(x_stored, at(t, 16, -16))
                sp.dma_start(xs[s][:, :, :], x_t[s, q]).then_inc(x_loaded[s], 16)

            def stack(t):
                sp.wait_ge(qlo_ready, at(t, KT, KT))
                sp.wait_ge(qhi_ready, at(t, KT, KT))
                for slot, src in enumerate((q_hi, q_lo, q_hi)):
                    for a in range(HPT):
                        sp.dma_start(qstack[DH * slot:DH * (slot + 1), a::HPT, :].bitcast(F32),
                                     src[DH * a:DH * (a + 1), :, :].bitcast(F32)).then_inc(stack_loaded, 16)

            def store(t, q, s):
                sp.wait_ge(out_ready, at(t, SUB, 2 * SUB))
                sp.dma_start(out_t[s, q], xs[s][:, :, :]).then_inc(x_stored, 16)

            load(None, 0, 0)
            load(None, 0, 1)
            stack(0)

            def tile(t, q, s, more=True, loads=True):
                if more:
                    stack(t + 1)
                store(t, q, s)
                if loads:
                    load(t + 2, q + 1, s)

            with sp.Fori(0, QT - 1) as i:
                for s in range(2):
                    tile(2 * i + s, i, s)
            for s in range(2):
                tile(NT - 2 + s, QT - 1, s, more=s == 0, loads=False)
            sp.wait_ge(x_stored, 16 * NT)

        @block.gpsimd
        def _(pool):
            n = 0

            def link(ins):
                nonlocal n
                n += 1
                ins.then_inc(pool_step, 1)
                pool.wait_ge(pool_step, n)

            consts = 0

            def ready(ins):
                nonlocal consts
                consts += 1
                ins.then_inc(const_ready, 1)
                pool.wait_ge(const_ready, consts)

            link(pool.memset(ident[:, :], 0.0))
            ready(pool.affine_select(out=ident[:, :], in_=ident[:, :], compare_op=ALU.not_equal, fill=1.0, base=0,
                                     pattern=[[-1, P]], channel_multiplier=1))
            ready(pool.memset(ones[:, :], 1.0))
            ready(pool.iota(tok[:, :], pattern=[[1, T]], base=0, channel_multiplier=0,
                      allow_small_or_imprecise_dtypes=True))
            ready(pool.iota(kcol[:, :], pattern=[[P, CC]], base=0, channel_multiplier=1,
                      allow_small_or_imprecise_dtypes=True))
            link(pool.memset(aux_f[64:96, :, :], 0.0))
            link(pool.affine_select(out=aux_f[64:96, :, :], in_=aux_f[64:96, :, :], compare_op=ALU.not_equal,
                                    fill=-1.0, base=0, pattern=[[-1, H], [0, J]], channel_multiplier=1))
            ready(pool.affine_select(out=aux_f[64:96, :, :], in_=aux_f[64:96, :, :], compare_op=ALU.not_equal,
                               fill=-1.0, base=-H, pattern=[[-1, H], [0, J]],
                               channel_multiplier=1))
            ready(pool.memset(kdiag_hi[:, :, :, :].bitcast(F32), 0.0))
            ready(pool.memset(kdiag_lo[:, :, :, :].bitcast(F32), 0.0))

            def root(t):
                pool.wait_ge(veps_ready, at(t, 1, 1))
                pool.tensor_tensor(rstd[:, :], veps[:, :], mhalf[:, :], ALU.pow).then_inc(rstd_ready, 1)

            pool.wait_ge(veps_ready, 1)
            pool.memset(mhalf[:, :], -0.5).then_inc(mhalf_ready, 1)
            pool.wait_ge(mhalf_ready, 1)
            root(0)
            with pool.Fori(1, NT) as t:
                root(t)

        @block.tensor
        def _(pe):
            def job(n):
                if n >= 8:
                    taken(pe, n - 8)
                return bank[n % 8]

            def turn_weight(n0, src, row0, k):
                b = job(n0 + k)
                for e in range(KT):
                    last = pe.transpose(b[:, e * P:(e + 1) * P], src[:, row0 + e, k * P:(k + 1) * P], ident[:, :])
                last.then_inc(job_done, 1)

            def product(n, terms, shape):
                b = job(n)
                for i, (l, r) in enumerate(terms):
                    last = pe.matmul(b[0:shape[0], 0:shape[1]], l, r, start=i == 0, stop=i == len(terms) - 1)
                last.then_inc(job_done, 1)

            pe.wait_ge(const_ready, 7)
            pe.wait_ge(s_vec, 16 * (NV + 2))
            b = job(JV)
            pe.wait_ge(cb_ready, 1)
            pe.transpose(b[:, 0:NV * KT], vrows[:, :], ident[0:NV * KT, 0:NV * KT])
            pe.transpose(b[:, NV * KT:NV * KT + CC], cb_f[:, :], ident[0:CC, 0:CC]).then_inc(job_done, 1)
            pe.wait_ge(s_ctx, 16)
            for n in range(2):
                b = job(JCTX + n)
                for kk in range(2):
                    for bb in range(B):
                        k = 2 * n + kk
                        last = pe.transpose(b[:, kk * BJ + bb * J:kk * BJ + (bb + 1) * J],
                                            ctx_sb[:, bb, k * P:(k + 1) * P], ident[0:J, 0:J])
                last.then_inc(job_done, 1)
            pe.wait_ge(s_wq, 16)
            for k in range(KT):
                turn_weight(JWQ, w_in_sb, 0, k)
            pe.wait_ge(s_wkv, 16)
            for k in range(KT):
                turn_weight(JWK, w_in_sb, KT, k)
            taken(pe, JWQ + 3)
            taken(pe, JWQ + 2)
            taken(pe, JV)
            b = job(JQB)
            for m in range(KT):
                for k in range(KT):
                    last = pe.matmul(b[:, m:m + 1], wT[:, 0, k, m * P:(m + 1) * P], vcol(V_BETA, k),
                                     start=k == 0, stop=k == KT - 1)
            last.then_inc(job_done, 1)
            taken(pe, JWK + 3)
            taken(pe, JWK + 2)
            taken(pe, JCTX)
            taken(pe, JCTX + 1)
            for m in range(KT):
                product(JK + m, [(wT[:, 1, k, m * P:(m + 1) * P], ctxT0[:, k, :]) for k in range(KT)], (P, BJ))
            for k in range(KT):
                turn_weight(JWV, w_in_sb, 2 * KT, k)
            taken(pe, JWV + 3)
            taken(pe, JWV + 2)
            for bb in range(B):
                product(JVV + bb, [(ctxT0[:, k, bb * J:(bb + 1) * J], wT[:, 0, k, :]) for k in range(KT)]
                        + [(ones[0:1, 0:J], bv_row[:, :])], (J, D))
            pe.wait_ge(s_w1, 16 * 5)
            for k in range(KT):
                turn_weight(JWO, w_out_sb, 0, k)
            for k in range(KT):
                turn_weight(JWQ1, wq1_sb, 0, k)
            for m in range(KT):
                product(JK1 + m, [(wk1_sb[:, k, m * P:(m + 1) * P], ctxT0[:, k, :]) for k in range(KT)], (P, BJ))
            for m in range(KT):
                product(JV1 + m, [(wv1_sb[:, k, m * P:(m + 1) * P], ctxT0[:, k, :]) for k in range(KT)], (P, BJ))
            taken(pe, JK1 + 3)
            taken(pe, JK1 + 2)
            for m in range(KT):
                product(JM + m, [(wT[:, 1, k, m * P:(m + 1) * P], k1T[:, k, :]) for k in range(KT)], (P, BJ))
            taken(pe, JM + 3)
            taken(pe, JM + 2)

            def mf(k):
                return m_f[:, k, :, :].rearrange("p b j -> p (b j)")

            for m in range(KT):
                product(JW2 + m, [(w_out_sb[:, k, m * P:(m + 1) * P], mf(k)) for k in range(KT)], (P, BJ))
            product(JCOL, [(ones[:, :], mf(k)) for k in range(KT)], (P, BJ))
            pe.wait_ge(rep_ready, 2 * KT)
            product(JC, [(rep[:, 0, k, :], mf(k)) for k in range(KT)]
                    + [(rep[:, 1, k, :], k1T[:, k, :]) for k in range(KT)], (P, BJ))
            taken(pe, JV1 + 3)
            taken(pe, JV1 + 2)
            for bb in range(B):
                product(JVW + bb, [(v1T[:, k, bb * J:(bb + 1) * J], wo1_sb[:, k, :]) for k in range(KT)], (J, D))
            pe.wait_ge(pick_ready, CC)
            b = job(JP)
            for c in range(CC):
                last = pe.matmul(b[:, 0:1], pick[:, c, :], cb_c[:, c:c + 1], start=c == 0, stop=c == CC - 1)
            last.then_inc(job_done, 1)
            for n in range(NJ - 8, NJ):
                taken(pe, n)
            pe.wait_ge(s_kstack, 16 * 3 * HPT * B)
            pe.wait_ge(s_bias1, 16 * 2 * B)
            pe.wait_ge(act_prepared, 1)
            pe.wait_ge(dve_prepared, 1)

            def turn_z(t, sub):
                pe.wait_ge(z_ready, at(t, SUB, sub + 1))
                if sub:
                    pe.wait_ge(zhi_ready, at(t, SUB, sub))
                    pe.wait_ge(zlo_ready, at(t, SUB, sub))
                for k in range(KT):
                    last = pe.transpose(bank[7][:, k * P:(k + 1) * P], z[:, sub % 2, k * P:(k + 1) * P], ident[:, :])
                last.then_inc(z_turned, 1)

            def split3(o, lhs, rhs, ks, more=0):
                n, total = 0, 3 * len(ks) + more
                for k in ks:
                    for l, r in ((0, 0), (0, 1), (1, 0)):
                        last = pe.matmul(o, lhs(l, k), rhs(r, k), start=n == 0, stop=n == total - 1)
                        n += 1
                return last

            wq = (wqT_hi, wqT_lo)
            wo = (woT_hi, woT_lo)
            zt = (zT_hi, zT_lo)
            aT = (attT_hi, attT_lo)
            qh = (q_hi, q_lo)
            kd = (kdiag_hi, kdiag_lo)
            mm = (m_hi, m_lo)
            w2 = (w2_hi, w2_lo)

            def project_q(t, s):
                pe.wait_ge(zlo_ready, at(t, SUB, SUB))
                pe.wait_ge(zhi_ready, at(t, SUB, SUB))
                for m in range(KT):
                    if m == 3:
                        pe.wait_ge(qlo_ready, at(t, KT, 1))
                        pe.wait_ge(qhi_ready, at(t, KT, 1))
                    split3(bank[m % 3][:, :], lambda l, k: wq[l][:, k, m * P:(m + 1) * P],
                           lambda r, k: zt[r][:, k, :], range(KT)).then_inc(q_done, 1)
                pe.wait_ge(qlo_ready, at(t, KT, 2))
                pe.wait_ge(qhi_ready, at(t, KT, 2))
                split3(bank[1][0:J, :], lambda l, k: mm[l][:, k, s, :],
                       lambda r, k: zt[r][:, k, :], range(KT)).then_inc(s1z_done, 1)

            def max_scores(t, s, subs):
                for sub in subs:
                    for g in range(KT):
                        u = sub * KT + g
                        if u < 3:
                            pe.wait_ge(qlo_ready, at(t, KT, KT))
                            pe.wait_ge(qhi_ready, at(t, KT, KT))
                            pe.wait_ge(s1z_ready, at(t, 1, 1))
                        else:
                            pe.wait_ge(max_taken, at(t, SUB * KT, u - 2))
                        split3(bank[u % 3][:, 0:GJ], lambda l, k: qh[l][:, g, sub * P:(sub + 1) * P],
                               lambda r, k: kd[r][:, s, g, :], [0]).then_inc(maxs_done, 1)

            def turn_max(t):
                pe.wait_ge(mx_ready, at(t, 1, 1))
                for sub in range(SUB):
                    last = pe.transpose(bank[0][0:2 * H, sub * P:(sub + 1) * P], mx2[:, sub, :], ident[:, :])
                last.then_inc(mx_turned, 1)

            def scores(t, q, s, h):
                if h == 0:
                    pe.wait_ge(auxq_ready, at(t, 1, 1))
                    pe.wait_ge(onehot_ready, at(q, 1, 1))
                    pe.wait_ge(stack_loaded, at(t, 16 * 3 * HPT, 16 * 3 * HPT))
                if h >= 3:
                    pe.wait_ge(prob_ready, at(t, H, h - 2))
                b = bank[h % 3][0:J, :]
                pe.matmul(b, kstack[:, s, h, :], qstack[:, h, :], start=True, stop=False)
                pe.matmul(b, auxw[:, h, :], auxq[:, :], start=False, stop=True).then_inc(scores_done, 1)

            def attend(t, s, h):
                g, a = h // HPT, h % HPT
                pe.wait_ge(prob_ready, at(t, H, h + 1))
                if a == 0 and g < 2:
                    pe.wait_ge(out_ready, at(t, SUB, 2 * g + 2))
                if a == 0 and g >= 2:
                    pe.wait_ge(att_ready, at(t, KT, g - 1))
                rows = slice(a * DH, (a + 1) * DH)
                pe.matmul(bank[3 + 2 * (g % 2)][rows, :], v0[:, s, h * DH:(h + 1) * DH], prob[:, h % 2, :],
                          start=True, stop=True)
                last = pe.matmul(bank[4 + 2 * (g % 2)][rows, :], ones[0:J, 0:DH], prob[:, h % 2, :],
                                 start=True, stop=True)
                last.then_inc(head_used, 1)

            def second_scores(t, s, more):
                if more:
                    pe.wait_ge(qlo_ready, at(t + 1, KT, 3))
                pe.wait_ge(attlo_ready, at(t, KT, KT))
                pe.wait_ge(atthi_ready, at(t, KT, KT))
                split3(bank[2][0:J, :], lambda l, k: w2[l][:, k, s, :],
                       lambda r, k: aT[r][:, k, :], range(KT)).then_inc(s1a_done, 1)

            def turn_second(t, s, more):
                if more:
                    pe.wait_ge(qlo_ready, at(t + 1, KT, KT))
                pe.wait_ge(s1z_ready, at(t, 1, 1))
                pe.wait_ge(s1a_ready, at(t, 1, 1))
                for sub in range(SUB):
                    pe.transpose(bank[7][:, sub * J:(sub + 1) * J], s1z[:, s, sub * P:(sub + 1) * P], ident[0:J, 0:J])
                for sub in range(SUB):
                    last = pe.transpose(bank[0][:, sub * J:(sub + 1) * J], s1t[0:J, sub * P:(sub + 1) * P],
                                        ident[0:J, 0:J])
                last.then_inc(s1_turned, 1)

            def out_proj(t, sub):
                b = bank[3 + sub]
                if sub == 0:
                    pe.wait_ge(att_ready, at(t, KT, KT))
                n = 0
                for k in range(KT):
                    for l, r in ((0, 0), (0, 1), (1, 0)):
                        pe.matmul(b[:, :], aT[l][:, k, sub * P:(sub + 1) * P], wo[r][:, k, :],
                                  start=n == 0, stop=False)
                        n += 1

            def turn_p1(t):
                pe.wait_ge(p1_ready, at(t, 1, 1))
                for sub in range(SUB):
                    last = pe.transpose(bank[7][0:J + 2, sub * P:(sub + 1) * P], p1[:, sub, :], ident[:, :])
                last.then_inc(p1_turned, 1)

            def second_out(t, s, sub):
                pe.wait_ge(p1T_ready, at(t, 1, 1))
                pe.matmul(bank[3 + sub][:, :], s1t[:, sub * P:(sub + 1) * P], vw1[:, s, :],
                          start=False, stop=True).then_inc(out_done, 1)

            for sub in range(SUB):
                turn_z(0, sub)
            project_q(0, 0)
            max_scores(0, 0, range(SUB))
            turn_max(0)

            def tile(t, q, s, more=True):
                n, ns = t + 1, 1 - s
                scores(t, q, s, 0)
                scores(t, q, s, 1)
                for h in range(H):
                    attend(t, s, h)
                    if h + 2 < H:
                        scores(t, q, s, h + 2)
                    if more and h in TURN_AT:
                        turn_z(n, TURN_AT.index(h))
                if more:
                    project_q(n, ns)
                second_scores(t, s, more)
                out_proj(t, 0)
                turn_second(t, s, more)
                out_proj(t, 1)
                if more:
                    pe.wait_ge(nmax1_ready, at(t, 1, 1))
                    max_scores(n, ns, range(SUB))
                turn_p1(t)
                out_proj(t, 2)
                if more:
                    turn_max(n)
                for sub in range(3):
                    second_out(t, s, sub)
                out_proj(t, 3)
                second_out(t, s, 3)

            with pe.Fori(0, QT - 1) as i:
                for s in range(2):
                    tile(2 * i + s, i, s)
            tile(NT - 2, QT - 1, 0)
            tile(NT - 1, QT - 1, 1, more=False)

        def takes(n):
            b = bank[n % 8]
            for j0, dst in ((JWQ, wT[:, 0]), (JWK, wT[:, 1]), (JWV, wT[:, 0]), (JWO, wT[:, 0]), (JWQ1, wT[:, 1])):
                if j0 <= n < j0 + KT:
                    return dst[:, n - j0, :], b[:, :], None, None
            if JCTX <= n < JCTX + 2:
                k = 2 * (n - JCTX)
                return ctxT0[:, k:k + 2, :].rearrange("p k j -> p (k j)"), b[:, 0:2 * BJ], None, None
            if JVV <= n < JVV + B:
                return v0[:, n - JVV, :], b[0:J, :], None, None
            if JVW <= n < JVW + B:
                return vw1[0:J, n - JVW, :], b[0:J, :], None, None
            for j0, dst, v, f in ((JK, kT, V_BK, None), (JK1, k1T, V_BK1, None), (JV1, v1T, V_BV1, None),
                                  (JM, m_f, None, SCALE1), (JW2, w2_f, None, None)):
                if j0 <= n < j0 + KT:
                    d = dst[:, n - j0]
                    if len(d.shape) == 3:
                        d = d.rearrange("p b j -> p (b j)")
                    return d, b[:, 0:BJ], None if v is None else vcol(v, n - j0), f
            if n == JCOL:
                return colm[:, :, :].rearrange("p b j -> p (b j)"), b[:, 0:BJ], None, None
            if n == JC:
                return cvec[:, :, :].rearrange("p b j -> p (b j)"), b[:, 0:BJ], None, None
            if n == JP:
                return ce_cs[:, :], b[:, 0:1], None, None

        @block.scalar
        def _(act):
            def take(n):
                act.wait_ge(job_done, n + 1)
                if n == JV:
                    act.activation(cb_c[:, :], bank[0][:, NV * KT:NV * KT + CC], ACT.Copy).then_inc(cb_ready, 1)
                    act.activation(vcols[:, :], bank[0][:, 0:NV * KT], ACT.Copy).then_inc(act_took, 1)
                    return
                dst, src, bias, factor = takes(n)
                if bias is not None:
                    act.wait_ge(act_took, 1)
                    act.activation(dst, src, ACT.Identity, bias=bias).then_inc(act_took, 1)
                else:
                    act.activation(dst, src, ACT.Copy, scale=1.0 if factor is None else factor)\
                       .then_inc(act_took, 1)

            for n in range(JV, JQB, 2):
                take(n)
            act.wait_ge(gs_ready, 1)
            for k in range(KT):
                taken(act, JWQ + k)
                act.activation(wqT_hi[:, k, :], wT[:, 0, k, :], ACT.Copy, scale=gs[:, k:k + 1]).then_inc(hi_done, 1)
            for n in range(JK, JK + KT, 2):
                take(n)
            for n in range(JK, JK + KT):
                taken(act, n)
            act.activation(kT_hi[:, :, :, :], kT[:, :, :, :], ACT.Copy).then_inc(hi_done, 1)
            act.wait_ge(wq_split, KT)
            for n in range(JWV, JWQ1, 2):
                take(n)
            for k in range(KT):
                taken(act, JWO + k)
                act.activation(woT_hi[:, k, :], wT[:, 0, k, :], ACT.Copy).then_inc(hi_done, 1)
            for n in range(JWQ1, JW2, 2):
                take(n)
            for n in range(JM, JM + KT):
                taken(act, n)
            act.activation(m_hi[:, :, :, :], m_f[:, :, :, :], ACT.Copy).then_inc(hi_done, 1)
            for n in range(JW2, JCOL, 2):
                take(n)
            for n in range(JW2, JW2 + KT):
                taken(act, n)
            act.activation(w2_hi[:, :, :, :], w2_f[:, :, :, :], ACT.Copy).then_inc(hi_done, 1)
            for n in range(JCOL, NJ - 1, 2):
                take(n)
            take(JP)
            act.wait_ge(act_took, NJ // 2 + 1)
            act.wait_ge(hi_done, 2 * KT + 3)
            act.activation(ce_cs2[:, :], ce_cs[:, :], ACT.Copy).then_inc(act_prepared, 1)

            def z_high(t, sub):
                act.wait_ge(z_turned, at(t, SUB, sub + 1))
                act.activation(zT_hi[:, :, sub * P:(sub + 1) * P],
                               bank[7][:, :].rearrange("p (k c) -> p k c", k=KT), ACT.Copy).then_inc(zhi_ready, 1)

            def q_high(t, s):
                for m in range(KT):
                    act.wait_ge(q_done, at(t, KT, m + 1))
                    act.activation(q_hi[:, m, :], bank[m % 3][:, :], ACT.Identity,
                                   bias=q_bias[:, m:m + 1]).then_inc(qhi_ready, 1)
                act.wait_ge(s1z_done, at(t, 1, 1))
                act.activation(s1z[:, s, :], bank[1][0:J, :], ACT.Copy).then_inc(s1z_ready, 1)

            def max_rows(t):
                act.wait_ge(mx_turned, at(t, 1, 1))
                act.activation(auxq[64:96, :], bank[0][0:2 * H, :], ACT.Copy).then_inc(auxq_ready, 1)

            def att_high(t, g):
                act.wait_ge(att_ready, at(t, KT, g + 1))
                act.activation(attT_hi[:, g, :], att[:, g % 2, :], ACT.Copy).then_inc(atthi_ready, 1)

            for sub in range(SUB):
                z_high(0, sub)
            q_high(0, 0)
            max_rows(0)

            def tile(t, s, more=True):
                n, ns = t + 1, 1 - s
                for h in range(H):
                    act.wait_ge(scores_done, at(t, H, h + 1))
                    if h >= 2:
                        act.wait_ge(head_used, at(t, H, h - 1))
                    act.activation(prob[:, h % 2, :], bank[h % 3][0:J, :], ACT.Exp).then_inc(prob_ready, 1)
                    if more and h - 2 in TURN_AT:
                        z_high(n, TURN_AT.index(h - 2))
                    if h % HPT == 2 and h > HPT:
                        att_high(t, h // HPT - 1)
                att_high(t, KT - 1)
                if more:
                    q_high(n, ns)
                act.wait_ge(s1a_done, at(t, 1, 1))
                act.activation(s1t[0:J, :], bank[2][0:J, :], ACT.Copy).then_inc(s1a_ready, 1)
                act.wait_ge(nmax1_ready, at(t, 1, 1))
                for sub in range(SUB):
                    act.activation(e1[:, sub, :], p1[:, sub, 0:J], ACT.Exp, bias=nmax1[:, sub:sub + 1],
                                   accum_out=sum1[:, sub:sub + 1]).then_inc(e1_ready, 1)
                act.wait_ge(p1_turned, at(t, 1, 1))
                act.activation(s1t[:, :], bank[7][0:J + 2, :], ACT.Copy).then_inc(p1T_ready, 1)
                if more:
                    max_rows(n)

            with act.Fori(0, QT - 1) as i:
                for s in range(2):
                    tile(2 * i + s, s)
            tile(NT - 2, 0)
            tile(NT - 1, 1, more=False)

        @block.vector
        def _(dve):
            nprep = 0

            def link(ins):
                nonlocal nprep
                nprep += 1
                ins.then_inc(prep_step, 1)
                dve.wait_ge(prep_step, nprep)

            def take(n):
                dve.wait_ge(job_done, n + 1)
                if n == JQB:
                    link(dve.tensor_tensor(q_bias[:, :], bank[n % 8][:, 0:KT],
                                           vcols[:, V_BQ * KT:(V_BQ + 1) * KT], ALU.add))
                    dve.tensor_scalar(q_bias[:, :], q_bias[:, :], SCALE0, None, ALU.mult).then_inc(dve_took, 1)
                    return
                dst, src, bias, factor = takes(n)
                if bias is not None:
                    dve.tensor_scalar(dst, src, bias, None, ALU.add).then_inc(dve_took, 1)
                elif factor is not None:
                    dve.tensor_scalar(dst, src, factor, None, ALU.mult).then_inc(dve_took, 1)
                else:
                    dve.tensor_copy(dst, src).then_inc(dve_took, 1)

            dve.wait_ge(s_vec, 16 * (NV + 2))
            dve.tensor_scalar(cb_f[:, :], cb_i[:, :], 0, J, ALU.max, ALU.min).then_inc(cb_ready, 1)
            for n in range(JV + 1, JQB, 2):
                take(n)
            taken(dve, JV)
            dve.tensor_scalar(gs[:, :], vcols[:, V_GAMMA * KT:(V_GAMMA + 1) * KT], SCALE0, None,
                              ALU.mult).then_inc(gs_ready, 1)
            dve.wait_ge(gs_ready, 1)
            for k in range(KT):
                dve.wait_ge(hi_done, k + 1)
                dve.scalar_tensor_tensor(out=wqT_lo[:, k, :], in0=wT[:, 0, k, :], scalar=gs[:, k:k + 1],
                                         in1=wqT_hi[:, k, :], op0=ALU.mult, op1=ALU.subtract).then_inc(wq_split, 1)
            take(JQB)
            for n in range(JK + 1, JK + KT, 2):
                take(n)
            dve.wait_ge(hi_done, KT + 1)
            dve.tensor_tensor(kT_lo[:, :, :, :], kT[:, :, :, :], kT_hi[:, :, :, :], ALU.subtract).then_inc(k_split, 1)
            for n in range(JWV + 1, JWQ1, 2):
                take(n)
            for k in range(KT):
                dve.wait_ge(hi_done, KT + 2 + k)
                dve.tensor_tensor(woT_lo[:, k, :], wT[:, 0, k, :], woT_hi[:, k, :],
                                  ALU.subtract).then_inc(wo_split, 1)
            for n in range(JWQ1 + 1, JM, 2):
                take(n)
            dve.wait_ge(const_ready, 7)
            for k in range(KT):
                dve.tensor_scalar(rep[:, 0, k, :], ones[:, :], vcol(V_BOUT, k), None, ALU.mult)\
                   .then_inc(rep_ready, 1)
                dve.tensor_scalar(rep[:, 1, k, :], ones[:, :], vcol(V_BQ1, k), SCALE1, ALU.mult, ALU.mult)\
                   .then_inc(rep_ready, 1)
            for n in range(JM + 1, JW2, 2):
                take(n)
            dve.wait_ge(hi_done, 2 * KT + 2)
            dve.tensor_tensor(m_lo[:, :, :, :], m_f[:, :, :, :], m_hi[:, :, :, :], ALU.subtract).then_inc(prep_lo, 1)
            dve.wait_ge(s_word, 16 * 7)
            link(dve.tensor_copy(wb32[:, :], wb_i[:, :]))
            dve.tensor_copy(widx[:, 0:W], wb32[:, 0:W])
            link(dve.tensor_scalar(widx[:, W:2 * W], wb32[:, 1:W + 1], 1.0, None, ALU.subtract))
            link(dve.tensor_scalar(widx2[:, :], widx[:, :], 0.0, float(NCB), ALU.is_lt, ALU.mult))
            link(dve.tensor_tensor(widx2[:, :], widx2[:, :], widx[:, :], ALU.add))
            link(dve.tensor_scalar(widx[:, :], widx2[:, :], 0.0, float(NCB - 1), ALU.max, ALU.min))
            for c in range(CC):
                dve.tensor_scalar(pick[:, c, :], widx[:, :], kcol[:, c:c + 1], None, ALU.is_equal)\
                   .then_inc(pick_ready, 1)
            for n in range(JW2 + 1, JCOL, 2):
                take(n)
            dve.wait_ge(hi_done, 2 * KT + 3)
            dve.tensor_tensor(w2_lo[:, :, :, :], w2_f[:, :, :, :], w2_hi[:, :, :, :], ALU.subtract).then_inc(prep_lo, 1)
            take(JC)
            take(JVW + 1)
            dve.wait_ge(k_split, 1)
            for b in range(B):
                for a in range(HPT):
                    rows = slice(DH * a, DH * (a + 1))
                    for dst, src in ((kdiag_hi, kT_hi), (kdiag_lo, kT_lo)):
                        dve.tensor_copy(dst[rows, b, :, a * J:(a + 1) * J], src[rows, :, b, :]).then_inc(prep_lo, 1)
            link(dve.tensor_copy(wcol[:, :], wcol_i[:, :]))
            taken(dve, JP)
            link(dve.tensor_copy(cend[:, :], ce_cs[W:2 * W, :]))
            link(dve.tensor_copy(wlo[:, :], wcol[:, 0:1]))
            link(dve.tensor_copy(whi[:, :], wcol[:, 1:2]))
            bounds = ((ce_cs[0:W, :], cend[:, :]), (wcol[:, 2:3], wcol[:, 0:1]), (wcol[:, 1:2], wcol[:, 3:4]))
            for r, (lo, hi) in enumerate(bounds):
                link(dve.tensor_scalar(ge[:, r, :], tok[:, 0:J], lo, None, ALU.is_ge))
                link(dve.scalar_tensor_tensor(out=rng[:, r, :], in0=tok[:, 0:J], scalar=hi, in1=ge[:, r, :],
                                              op0=ALU.is_lt, op1=ALU.mult))
            link(dve.tensor_tensor(rng[:, 0, :], rng[:, 0, :], rng[:, 1, :], ALU.max))
            link(dve.tensor_tensor(rng[:, 0, :], rng[:, 0, :], rng[:, 2, :], ALU.max))
            for h in range(H):
                dve.tensor_copy(auxw[0:W, h, :], rng[:, 0, :]).then_inc(prep_lo, 1)
            dve.tensor_copy(auxw[64:96, :, :], aux_f[64:96, :, :]).then_inc(prep_lo, 1)
            dve.wait_ge(prep_lo, 2 + 4 * B * HPT // 2 + H + 1)
            dve.wait_ge(wo_split, KT)
            dve.wait_ge(dve_took, NJ // 2)
            dve.memset(p1ones[:, :], 1.0).then_inc(out_ready, SUB)
            dve.wait_ge(out_ready, SUB)
            dve.tensor_copy(dve_mark[:, :], p1ones[:, 0:1]).then_inc(dve_prepared, 1)

            cnt = [0]
            base = [0]

            def count(ins):
                cnt[0] += 1
                ins.then_inc(step, 1)

            def own(ins):
                count(ins)
                dve.wait_ge(step, base[0] + cnt[0])

            def normalise(t, q, s):
                dve.wait_ge(x_loaded[s], at(q, 16, 16))
                for sub in range(SUB):
                    ins = dve.bn_stats(stats[:, sub, :], xs[s][:, sub, :])
                    if sub < SUB - 1:
                        count(ins)
                own(ins)
                even, odd = stats[:, :, 0:3], stats[:, :, 3:6]
                count(dve.tensor_tensor(mean[s][:, :], even[:, :, 1], odd[:, :, 1], ALU.add))
                count(dve.tensor_tensor(mdiff[:, :], even[:, :, 1], odd[:, :, 1], ALU.subtract))
                own(dve.tensor_tensor(veps[:, :], even[:, :, 2], odd[:, :, 2], ALU.add))
                count(dve.tensor_scalar(mean[s][:, :], mean[s][:, :], 0.5, None, ALU.mult))
                count(dve.tensor_tensor(mdiff[:, :], mdiff[:, :], mdiff[:, :], ALU.mult))
                own(dve.tensor_scalar(veps[:, :], veps[:, :], 1.0 / D, EPS, ALU.mult, ALU.add))
                dve.scalar_tensor_tensor(out=veps[:, :], in0=mdiff[:, :], scalar=0.25, in1=veps[:, :],
                                         op0=ALU.mult, op1=ALU.add).then_inc(veps_ready, 1)
                dve.wait_ge(rstd_ready, at(t, 1, 1))
                own(dve.reciprocal(std[s][:, :], rstd[:, :]))

            def z_part(t, s, sub):
                if sub >= 2:
                    dve.wait_ge(z_turned, at(t, SUB, sub - 1))
                dve.tensor_scalar(z[:, sub % 2, :], xs[s][:, sub, :], mean[s][:, sub:sub + 1], rstd[:, sub:sub + 1],
                                  ALU.subtract, ALU.mult).then_inc(z_ready, 1)

            def z_low(t, sub):
                dve.wait_ge(zhi_ready, at(t, SUB, sub + 1))
                part = slice(sub * P, (sub + 1) * P)
                dve.tensor_tensor(zT_lo[:, :, part], bank[7][:, :].rearrange("p (k c) -> p k c", k=KT),
                                  zT_hi[:, :, part], ALU.subtract).then_inc(zlo_ready, 1)

            def q_low(t):
                for m in range(KT):
                    dve.wait_ge(qhi_ready, at(t, KT, m + 1))
                    dve.scalar_tensor_tensor(out=q_lo[:, m, :], in0=bank[m % 3][:, :], scalar=q_bias[:, m:m + 1],
                                             in1=q_hi[:, m, :], op0=ALU.add, op1=ALU.subtract).then_inc(qlo_ready, 1)

            def take_max(t, us):
                for u in us:
                    sub, g = u // KT, u % KT
                    dve.wait_ge(maxs_done, at(t, SUB * KT, u + 1))
                    dve.tensor_reduce(mx[:, sub, g * HPT:(g + 1) * HPT],
                                      bank[u % 3][:, 0:GJ].rearrange("p (a j) -> p a j", a=HPT), AX.X,
                                      ALU.max).then_inc(max_taken, 1)

            def split_max(t):
                dve.wait_ge(max_taken, at(t, SUB * KT, SUB * KT))
                own(dve.tensor_copy(mx_hr[:, :, :], mx[:, :, :]))
                own(dve.tensor_copy(mx2[:, :, 0:H], mx_hr[:, :, :]))
                dve.tensor_tensor(mx2[:, :, H:2 * H], mx[:, :, :], mx_hr[:, :, :], ALU.subtract).then_inc(mx_ready, 1)

            def one_hot():
                own(dve.tensor_scalar(att[0:W, 0, :], tok[:, :], wlo[:, :], None, ALU.is_ge))
                dve.scalar_tensor_tensor(out=auxq[0:W, :], in0=tok[:, :], scalar=whi[:, :], in1=att[0:W, 0, :],
                                         op0=ALU.is_lt, op1=ALU.mult).then_inc(onehot_ready, 1)

            def divide(t, g):
                dve.wait_ge(head_used, at(t, H, HPT * (g + 1)))
                own(dve.reciprocal(att[:, g % 2, :], bank[4 + 2 * (g % 2)][:, :]))
                dve.tensor_tensor(att[:, g % 2, :], bank[3 + 2 * (g % 2)][:, :], att[:, g % 2, :],
                                  ALU.mult).then_inc(att_ready, 1)

            def att_low(t, g):
                dve.wait_ge(atthi_ready, at(t, KT, g + 1))
                dve.tensor_tensor(attT_lo[:, g, :], att[:, g % 2, :], attT_hi[:, g, :],
                                  ALU.subtract).then_inc(attlo_ready, 1)

            normalise(0, 0, 0)
            z_part(0, 0, 0)
            z_part(0, 0, 1)
            z_low(0, 0)
            z_part(0, 0, 2)
            z_low(0, 1)
            z_part(0, 0, 3)
            z_low(0, 2)
            z_low(0, 3)
            q_low(0)
            one_hot()
            take_max(0, range(SUB * KT))
            split_max(0)
            own(dve.memset(p1[:, :, J:J + 2], 1.0))
            first = cnt[0]
            NSTEP = 2 * (SUB + 6 + 1 + 2 * SUB + 1 + SUB + 2 + KT) + 3

            def tile(t, q, s, more=True):
                n, ns, nq = t + 1, 1 - s, q + s
                divide(t, 0)
                if more:
                    normalise(n, nq, ns)
                    z_part(n, ns, 0)
                    z_part(n, ns, 1)
                att_low(t, 0)
                divide(t, 1)
                if more:
                    z_low(n, 0)
                    z_part(n, ns, 2)
                att_low(t, 1)
                if more:
                    z_low(n, 1)
                    z_part(n, ns, 3)
                divide(t, 2)
                if more:
                    z_low(n, 2)
                att_low(t, 2)
                if more:
                    z_low(n, 3)
                divide(t, 3)
                att_low(t, 3)
                if more:
                    q_low(n)
                for sub in range(SUB):
                    own(dve.scalar_tensor_tensor(out=sc1b[:, sub, :], in0=colm[:, s, :], scalar=mean[s][:, sub:sub + 1],
                                                 in1=cvec[:, s, :], op0=ALU.mult, op1=ALU.add))
                dve.wait_ge(s1_turned, at(t, 1, 1))
                for sub in range(SUB):
                    own(dve.scalar_tensor_tensor(out=sc1b[:, sub, :], in0=bank[7][:, sub * J:(sub + 1) * J],
                                                 scalar=std[s][:, sub:sub + 1], in1=sc1b[:, sub, :],
                                                 op0=ALU.mult, op1=ALU.add))
                own(dve.tensor_tensor(sc1, sc1b[:, :, :],
                                      bank[0][:, 0:SUB * J].rearrange("p (s j) -> p s j", s=SUB), ALU.add))
                dve.tensor_reduce(nmax1[:, :], sc1, AX.X, ALU.max, negate=True).then_inc(nmax1_ready, 1)
                if more:
                    take_max(n, range(2 * KT))
                dve.wait_ge(e1_ready, at(t, SUB, SUB))
                own(dve.reciprocal(rsum1[:, :], sum1[:, :]))
                for sub in range(SUB):
                    ins = dve.tensor_scalar(p1[:, sub, 0:J], e1[:, sub, :], rsum1[:, sub:sub + 1], None, ALU.mult)
                    if sub < SUB - 1:
                        own(ins)
                    else:
                        ins.then_inc(p1_ready, 1)
                if more:
                    take_max(n, range(2 * KT, SUB * KT))
                    split_max(n)
                    if s == 1:
                        own(dve.tensor_scalar(wlo[:, :], wlo[:, :], float(T), None, ALU.subtract))
                        own(dve.tensor_scalar(whi[:, :], whi[:, :], float(T), None, ALU.subtract))
                        one_hot()
                for sub in range(SUB):
                    dve.wait_ge(out_done, at(t, SUB, sub + 1))
                    dve.tensor_tensor(xs[s][:, sub, :], bank[3 + sub][:, :], xs[s][:, sub, :],
                                      ALU.add).then_inc(out_ready, 1)

            with dve.Fori(0, QT - 1) as i:
                base[0] = i * NSTEP + first
                cnt[0] = 0
                for s in range(2):
                    tile(2 * i + s, i, s)
                assert cnt[0] == NSTEP, cnt[0]
            base[0] = (QT - 1) * NSTEP + first
            cnt[0] = 0
            tile(NT - 2, QT - 1, 0)
            tile(NT - 1, QT - 1, 1, more=False)


_INS = ["x", "ctx_1024", "itok_S_0_4092", "L0_xattn_word_boundaries", "L0_xattn_ln_gamma", "L0_xattn_ln_beta",
        "L0_xattn_in_proj_w", "L0_xattn_in_proj_b", "L0_xattn_out_w", "L0_xattn_out_b",
        "L1_xattn_Wq", "L1_xattn_bq", "L1_xattn_Wk", "L1_xattn_bk", "L1_xattn_Wv", "L1_xattn_bv",
        "L1_xattn_Wo", "L1_xattn_bo"]


def kernel(**inputs):
    import numpy as _np
    import concourse.bacc as _bacc
    from concourse import mybir as _mybir
    from concourse.bass_utils import run_bass_kernel_spmd as _run

    nc = _bacc.Bacc("TRN2", target_bir_lowering=False, num_devices=1)
    arrays, args = {}, []
    for name in _INS:
        a = _np.ascontiguousarray(inputs[name])
        arrays[f"in_{name}_dram"] = a
        args.append(nc.dram_tensor(f"in_{name}_dram", a.shape, _mybir.dt.from_np(a.dtype), kind="ExternalInput").ap())
    shape = tuple(inputs["x"].shape)
    args.append(nc.dram_tensor("out_0_dram", shape, _mybir.dt.float32, kind="ExternalOutput").ap())
    two_cross_attentions(nc, *args)
    r = _run(nc, [arrays], core_ids=[0])
    return r.results[0]["out_0_dram"]
```

```python
from contextlib import ExitStack

import concourse.bass as bass
from concourse import mybir

ALU = mybir.AluOpType
ACT = mybir.ActivationFunctionType
AX = mybir.AxisListType
F32 = mybir.dt.float32
F32R = mybir.dt.float32r
F16 = mybir.dt.float16
BF16 = mybir.dt.bfloat16
I32 = mybir.dt.int32

P = 128
EPS = 1e-5


def two_cross_attentions(
    nc: bass.Bass,
    x: bass.AP,
    ctx_in: bass.AP,
    char_bounds: bass.AP,
    word_bounds: bass.AP,
    gamma: bass.AP,
    beta: bass.AP,
    w_in: bass.AP,
    b_in: bass.AP,
    w_out: bass.AP,
    b_out: bass.AP,
    wq1: bass.AP,
    bq1: bass.AP,
    wk1: bass.AP,
    bk1: bass.AP,
    wv1: bass.AP,
    bv1: bass.AP,
    wo1: bass.AP,
    bo1: bass.AP,
    out: bass.AP,
):
    B, S, D = x.shape
    J = ctx_in.shape[1]
    H = 16
    DH = D // H
    KT = D // P
    HPT = P // DH
    W = word_bounds.shape[0] - 1
    T = 512
    SUB = T // P
    QT = S // T
    NT = B * QT
    NCB = char_bounds.shape[0]
    CC = NCB // P
    SCALE0 = float(DH) ** -0.5
    SCALE1 = float(D // 8) ** -0.5
    GJ = HPT * J
    BJ = B * J
    NV = 8
    assert B == 2 and D == 512 and J <= 77 and W == 64 and CC == 16 and DH == 32

    x_t = x.rearrange("b (q s p) d -> b q p s d", s=SUB, p=P)
    out_t = out.rearrange("b (q s p) d -> b q p s d", s=SUB, p=P)

    with ExitStack() as ctx:
        def sem(name):
            return ctx.enter_context(nc.semaphore(name))

        def keep(name, shape, dt):
            return ctx.enter_context(nc.sbuf_tensor(name, shape, dt))

        wqT_hi = keep("wqT_hi", [P, KT, D], F32R)
        wqT_lo = keep("wqT_lo", [P, KT, D], F32R)
        woT_hi = keep("woT_hi", [P, KT, D], F32R)
        woT_lo = keep("woT_lo", [P, KT, D], F32R)
        kdiag_hi = keep("kdiag_hi", [P, B, KT, GJ], F32R)
        kdiag_lo = keep("kdiag_lo", [P, B, KT, GJ], F32R)
        kstack = keep("kstack", [P, B, H, J], F32R)
        maskw = keep("maskw", [P, J], F32R)
        densel = keep("densel", [J, KT, DH], F32)
        v0 = keep("v0", [J, B, D], F32)
        vw1 = keep("vw1", [J + 2, B, D], F32)
        m_hi = keep("m_hi", [P, KT, B, J], F32R)
        m_lo = keep("m_lo", [P, KT, B, J], F32R)
        w2_hi = keep("w2_hi", [P, KT, B, J], F32R)
        w2_lo = keep("w2_lo", [P, KT, B, J], F32R)
        colm = keep("colm", [P, B, J], F32)
        cvec = keep("cvec", [P, B, J], F32)
        ident = keep("ident", [P, P], F32)
        ones = keep("ones", [P, P], F32)
        q_bias = keep("q_bias", [P, KT], F32)
        tok = keep("tok", [W, T], F16)
        wlo = keep("wlo", [W, 1], F32)
        whi = keep("whi", [W, 1], F32)
        vcols = keep("vcols", [P, NV * KT], F32)

        bank = [ctx.enter_context(nc.psum_tensor(f"bank{i}", [P, 512], F32)) for i in range(8)]

        with ExitStack() as prep:
            def tmp(name, shape, dt):
                return prep.enter_context(nc.sbuf_tensor(name, shape, dt))

            w_in_sb = tmp("w_in_sb", [P, 3 * KT, D], F32)
            w_out_sb = tmp("w_out_sb", [P, KT, D], F32)
            wq1_sb = tmp("wq1_sb", [P, KT, D], F32)
            wk1_sb = tmp("wk1_sb", [P, KT, D], F32)
            wv1_sb = tmp("wv1_sb", [P, KT, D], F32)
            wo1_sb = w_in_sb[:, 0:KT, :]
            ctx_sb = tmp("ctx_sb", [J, B, D], F32)
            ctxT0 = tmp("ctxT0", [P, KT, BJ], F32)
            wT = tmp("wT", [P, 2, KT, D], F32)
            kT = tmp("kT", [P, KT, B, J], F32)
            kT_hi = tmp("kT_hi", [P, KT, B, J], F32R)
            kT_lo = tmp("kT_lo", [P, KT, B, J], F32R)
            k1T = tmp("k1T", [P, KT, BJ], F32)
            v1T = tmp("v1T", [P, KT, BJ], F32)
            m_f = tmp("m_f", [P, KT, B, J], F32)
            w2_f = tmp("w2_f", [P, KT, B, J], F32)
            vrows = tmp("vrows", [NV * KT, P], F32)
            rep = tmp("rep", [P, 2, KT, P], F32)
            bv_row = tmp("bv_row", [1, D], F32)
            gs = tmp("gs", [P, KT], F32)
            cb_i = tmp("cb_i", [CC, P], I32)
            cb_f = tmp("cb_f", [CC, P], F32)
            cb_c = tmp("cb_c", [P, CC], BF16)
            wb_i = tmp("wb_i", [P, W + 1], I32)
            widx = tmp("widx", [P, 2 * W], F32)
            widx2 = tmp("widx2", [P, 2 * W], F32)
            kcol = tmp("kcol", [P, CC], F32)
            pick = tmp("pick", [P, CC, 2 * W], BF16)
            wcol_i = tmp("wcol_i", [W, 4], I32)
            wcol = tmp("wcol", [W, 4], F32)
            ce_cs = tmp("ce_cs", [P, 1], F32)
            ce_cs2 = tmp("ce_cs2", [P, 1], F32)
            p1ones = tmp("p1ones", [P, 2], F32)
            dve_mark = tmp("dve_mark", [P, 1], F32)
            cend = tmp("cend", [W, 1], F32)
            ge = tmp("ge", [W, 3, J], F32)
            rng = tmp("rng", [W, 3, J], F32)
            msel = tmp("msel", [P, H, J], F32)
            wb32 = tmp("wb32", [P, W + 1], F32)

        xs = [keep(f"x{i}", [P, SUB, D], F32) for i in range(2)]
        zT_hi = keep("zT_hi", [P, KT, T], F32R)
        zT_lo = keep("zT_lo", [P, KT, T], F32R)
        q_hi = keep("q_hi", [P, KT, T], F32R)
        q_lo = keep("q_lo", [P, KT, T], F32R)
        qstack = keep("qstack", [P, H, T], F32R)
        onehot = keep("onehot", [P, T], F32R)
        prob = keep("prob", [J, 6, T], F32)
        mrows = prob[0:2 * H, 0, :]
        s1t_rd = keep("s1t_rd", [P, T], F32)
        rd = s1t_rd[:, :]
        s1t = s1t_rd[0:J + 2, :]
        att = keep("att", [P, 2, T], F32)
        z = att
        attT_hi = keep("attT_hi", [P, KT, T], F32R)
        attT_lo = keep("attT_lo", [P, KT, T], F32R)
        s1z = keep("s1z", [J, 2, T], F32)
        stats = keep("stats", [P, SUB, 6], F32)
        mean = [keep(f"mean{i}", [P, SUB], F32) for i in range(2)]
        mdiff = keep("mdiff", [P, SUB], F32)
        veps = keep("veps", [P, SUB], F32)
        mhalf = keep("mhalf", [P, SUB], F32)
        rstd = keep("rstd", [P, SUB], F32)
        std = [keep(f"std{i}", [P, SUB], F32) for i in range(2)]
        mx = keep("mx", [P, SUB, H], F32)
        mx_hr = keep("mx_hr", [P, SUB, H], F32R)
        mx2 = keep("mx2", [P, SUB, 2 * H], F32)
        p1 = keep("p1", [P, SUB, J + 2], F32)
        sc1 = p1[:, :, 0:J]
        sc1b = keep("sc1b", [P, SUB, J], F32)
        nmax1 = keep("nmax1", [P, SUB], F32)
        sum1 = keep("sum1", [P, SUB], F32)
        rsum1 = keep("rsum1", [P, SUB], F32)
        e1 = sc1b

        s_vec = sem("s_vec")
        s_word = sem("s_word")
        s_ctx = sem("s_ctx")
        s_wq = sem("s_wq")
        s_wkv = sem("s_wkv")
        s_w1 = sem("s_w1")
        s_bias1 = sem("s_bias1")
        s_kstack = sem("s_kstack")
        const_ready = sem("const_ready")
        job_done = sem("job_done")
        act_took = sem("act_took")
        dve_took = sem("dve_took")
        pool_step = sem("pool_step")
        cb_ready = sem("cb_ready")
        gs_ready = sem("gs_ready")
        hi_done = sem("hi_done")
        wo_split = sem("wo_split")
        prep_lo = sem("prep_lo")
        wq_split = sem("wq_split")
        k_split = sem("k_split")
        prep_step = sem("prep_step")
        rep_ready = sem("rep_ready")
        pick_ready = sem("pick_ready")
        act_prepared = sem("act_prepared")
        dve_prepared = sem("dve_prepared")
        x_loaded = [[sem(f"x_loaded{i}_{sub}") for sub in range(SUB)] for i in range(2)]
        x_stored = [sem(f"x_stored{sub}") for sub in range(SUB)]
        stack_loaded = sem("stack_loaded")
        step = sem("step")
        veps_ready = sem("veps_ready")
        rstd_ready = sem("rstd_ready")
        z_ready = sem("z_ready")
        z_turned = sem("z_turned")
        zhi_ready = sem("zhi_ready")
        zlo_ready = sem("zlo_ready")
        q_done = sem("q_done")
        qhi_ready = sem("qhi_ready")
        qlo_ready = sem("qlo_ready")
        s1z_done = sem("s1z_done")
        s1z_ready = sem("s1z_ready")
        maxs_done = sem("maxs_done")
        max_taken = sem("max_taken")
        mx_ready = sem("mx_ready")
        mx_turned = sem("mx_turned")
        mrows_ready = sem("mrows_ready")
        mrows_spread = sem("mrows_spread")
        pads_ready = sem("pads_ready")
        rd_ready = sem("rd_ready")
        onehot_ready = sem("onehot_ready")
        scores_done = sem("scores_done")
        prob_ready = sem("prob_ready")
        group_used = sem("group_used")
        att_ready = sem("att_ready")
        atthi_ready = sem("atthi_ready")
        attlo_ready = sem("attlo_ready")
        s1a_done = sem("s1a_done")
        s1a_ready = sem("s1a_ready")
        s1_turned = sem("s1_turned")
        nmax1_ready = sem("nmax1_ready")
        e1_ready = sem("e1_ready")
        p1_ready = sem("p1_ready")
        p1_turned = sem("p1_turned")
        p1T_ready = sem("p1T_ready")
        out_done = sem("out_done")
        out_ready = sem("out_ready")

        def at(t, per, c):
            return t * per + c

        JV = 0
        JCTX = 1
        JWQ = 3
        JWK = JWQ + KT
        JQB = JWK + KT
        JK = JQB + 1
        JWV = JK + KT
        JVV = JWV + KT
        JWO = JVV + B
        JWQ1 = JWO + KT
        JK1 = JWQ1 + KT
        JV1 = JK1 + KT
        JM = JV1 + KT
        JW2 = JM + KT
        JCOL = JW2 + KT
        JC = JCOL + 1
        JVW = JC + 1
        JP = JVW + B
        NJ = JP + 1
        NCONST = 8 + KT
        AHEAD = 2
        NPROB = HPT + AHEAD
        SCORE_BANKS = [(0, 1, 7)[h % 3] for h in range(H - HPT)] + [0, 1] * (HPT // 2)
        TURN_BANKS = (7, 7, 0, 1)
        MAX_BANKS = (2, 7, 0, 1)
        V_BQ, V_BK, V_GAMMA, V_BETA, V_BOUT, V_BQ1, V_BK1, V_BV1 = range(NV)

        def taken(eng, n):
            if n % 2 == 0:
                eng.wait_ge(act_took, n // 2 + 1)
            else:
                eng.wait_ge(dve_took, n // 2 + 1)

        def vcol(v, k):
            return vcols[:, v * KT + k:v * KT + k + 1]

        block = ctx.enter_context(nc.Block())

        @block.sync
        def _(sp):
            vecs = [b_in[0:D], b_in[D:2 * D], gamma, beta, b_out, bq1, bk1, bv1]
            for n, v in enumerate(vecs):
                sp.dma_start(vrows[n * KT:(n + 1) * KT, :], v.rearrange("(k p) -> k p", p=P)).then_inc(s_vec, 16)
            sp.dma_start(cb_i[:, :], char_bounds.rearrange("(c p) -> c p", p=P)).then_inc(s_vec, 16)
            sp.dma_start(ctx_sb[:, :, :], ctx_in.rearrange("b j d -> j b d")).then_inc(s_ctx, 16)
            w_in_v = w_in.rearrange("(t p) d -> p t d", p=P)
            sp.dma_start(w_in_sb[:, 0:KT, :], w_in_v[:, 0:KT, :]).then_inc(s_wq, 16)
            wb = word_bounds.rearrange("(w o) -> w o", o=1)
            with nc.allow_non_contiguous_dma(reason="65 word boundaries, one per partition"):
                for dst, src in (((0, W, 0), (0, W)), ((0, W, 1), (1, W + 1)),
                                 ((0, 1, 2), (0, 1)), ((1, W, 2), (0, W - 1)),
                                 ((0, W - 1, 3), (2, W + 1)), ((W - 1, W, 3), (W, W + 1))):
                    sp.dma_start(wcol_i[dst[0]:dst[1], dst[2]:dst[2] + 1], wb[src[0]:src[1], :]).then_inc(s_word, 16)
            sp.dma_start(wb_i[:, :], word_bounds.rearrange("(o w) -> o w", o=1).broadcast_to([P, W + 1])).then_inc(s_word, 16)
            sp.dma_start(bv_row[:, :], b_in[2 * D:3 * D].rearrange("(o d) -> o d", o=1)).then_inc(s_vec, 16)
            sp.dma_start(w_in_sb[:, KT:3 * KT, :], w_in_v[:, KT:3 * KT, :]).then_inc(s_wkv, 16)
            for dst, src in ((w_out_sb, w_out), (wq1_sb, wq1), (wk1_sb, wk1), (wv1_sb, wv1), (wo1_sb, wo1)):
                if dst is wo1_sb:
                    sp.wait_ge(job_done, JWQ + KT)
                sp.dma_start(dst[:, :, :], src.rearrange("(t p) d -> p t d", p=P)).then_inc(s_w1, 16)
            for b in range(B):
                sp.dma_start(vw1[J:J + 1, b, :], bo1.rearrange("(o d) -> o d", o=1)).then_inc(s_bias1, 16)
                sp.dma_start(vw1[J + 1:J + 2, b, :], b_out.rearrange("(o d) -> o d", o=1)).then_inc(s_bias1, 16)
            sp.wait_ge(k_split, 1)
            for slot, src in enumerate((kT_hi, kT_hi, kT_lo)):
                for a in range(HPT):
                    for b in range(B):
                        sp.dma_start(kstack[DH * slot:DH * (slot + 1), b, a::HPT, :].bitcast(F32),
                                     src[DH * a:DH * (a + 1), :, b, :].bitcast(F32)).then_inc(s_kstack, 16)
            sp.wait_ge(s_kstack, 16 * 3 * HPT * B)
            sp.wait_ge(job_done, NJ)
            sp.wait_ge(act_prepared, 1)
            sp.wait_ge(dve_prepared, 1)

            def load(t_prev, q, s):
                for sub in range(SUB):
                    if t_prev is not None:
                        sp.wait_ge(x_stored[sub], at(t_prev, 16, 16))
                    sp.dma_start(xs[s][:, sub, :], x_t[s, q, :, sub]).then_inc(x_loaded[s][sub], 16)

            def stack(t):
                sp.wait_ge(qlo_ready, at(t, KT, KT))
                sp.wait_ge(qhi_ready, at(t, KT, KT))
                for slot, src in enumerate((q_hi, q_lo, q_hi)):
                    for a in range(HPT):
                        sp.dma_start(qstack[DH * slot:DH * (slot + 1), a::HPT, :].bitcast(F32),
                                     src[DH * a:DH * (a + 1), :, :].bitcast(F32)).then_inc(stack_loaded, 16)

            def spread_max(t):
                sp.wait_ge(mrows_ready, at(t, 1, 1))
                sp.dma_start(qstack[96:P, :, :].bitcast(F32),
                             mrows.unsqueeze(1).broadcast_to([2 * H, H, T])).then_inc(mrows_spread, 16)

            def store(t, q, s):
                for sub in range(SUB):
                    sp.wait_ge(out_ready, at(t, SUB, SUB + sub + 1))
                    sp.dma_start(out_t[s, q, :, sub], xs[s][:, sub, :]).then_inc(x_stored[sub], 16)

            load(None, 0, 0)
            load(None, 0, 1)
            stack(0)
            spread_max(0)

            def tile(t, q, s, more=True, loads=True):
                if more:
                    stack(t + 1)
                    spread_max(t + 1)
                store(t, q, s)
                if loads:
                    load(t, q + 1, s)

            with sp.Fori(0, QT - 1) as i:
                for s in range(2):
                    tile(2 * i + s, i, s)
            for s in range(2):
                tile(NT - 2 + s, QT - 1, s, more=s == 0, loads=False)
            for sub in range(SUB):
                sp.wait_ge(x_stored[sub], 16 * NT)

        @block.gpsimd
        def _(pool):
            n = 0

            def link(ins):
                nonlocal n
                n += 1
                ins.then_inc(pool_step, 1)
                pool.wait_ge(pool_step, n)

            consts = 0

            def ready(ins):
                nonlocal consts
                consts += 1
                ins.then_inc(const_ready, 1)
                pool.wait_ge(const_ready, consts)

            link(pool.memset(ident[:, :], 0.0))
            ready(pool.affine_select(out=ident[:, :], in_=ident[:, :], compare_op=ALU.not_equal, fill=1.0, base=0,
                                     pattern=[[-1, P]], channel_multiplier=1))
            ready(pool.memset(ones[:, :], 1.0))
            ready(pool.iota(tok[:, :], pattern=[[1, T]], base=0, channel_multiplier=0,
                      allow_small_or_imprecise_dtypes=True))
            ready(pool.iota(kcol[:, :], pattern=[[P, CC]], base=0, channel_multiplier=1,
                      allow_small_or_imprecise_dtypes=True))
            link(pool.memset(msel[96:P, :, :], 0.0))
            link(pool.affine_select(out=msel[96:P, :, :], in_=msel[96:P, :, :], compare_op=ALU.not_equal,
                                    fill=-1.0, base=0, pattern=[[-1, H], [0, J]], channel_multiplier=1))
            ready(pool.affine_select(out=msel[96:P, :, :], in_=msel[96:P, :, :], compare_op=ALU.not_equal,
                                     fill=-1.0, base=-H, pattern=[[-1, H], [0, J]], channel_multiplier=1))
            link(pool.memset(densel[:, :, :], 0.0))
            for g in range(KT):
                ready(pool.memset(densel[:, g, g::KT], 1.0))
            ready(pool.memset(maskw[64:P, :].bitcast(F32), 0.0))
            ready(pool.memset(kdiag_hi[:, :, :, :].bitcast(F32), 0.0))
            ready(pool.memset(kdiag_lo[:, :, :, :].bitcast(F32), 0.0))

            def root(t):
                pool.wait_ge(veps_ready, at(t, 1, 1))
                pool.tensor_tensor(rstd[:, :], veps[:, :], mhalf[:, :], ALU.pow).then_inc(rstd_ready, 1)

            pool.wait_ge(veps_ready, 1)
            pool.memset(mhalf[:, :], -0.5).then_inc(pads_ready, 1)
            pool.wait_ge(pads_ready, 1)
            pool.memset(onehot[64:P, :].bitcast(F32), 0.0).then_inc(pads_ready, 1)
            pool.wait_ge(pads_ready, 2)
            root(0)
            with pool.Fori(1, NT) as t:
                root(t)

        @block.tensor
        def _(pe):
            def job(n):
                if n >= 8:
                    taken(pe, n - 8)
                return bank[n % 8]

            def turn_weight(n0, src, row0, k):
                b = job(n0 + k)
                for e in range(KT):
                    last = pe.transpose(b[:, e * P:(e + 1) * P], src[:, row0 + e, k * P:(k + 1) * P], ident[:, :])
                last.then_inc(job_done, 1)

            def product(n, terms, shape):
                b = job(n)
                for i, (l, r) in enumerate(terms):
                    last = pe.matmul(b[0:shape[0], 0:shape[1]], l, r, start=i == 0, stop=i == len(terms) - 1)
                last.then_inc(job_done, 1)

            pe.wait_ge(const_ready, NCONST)
            pe.wait_ge(s_vec, 16 * (NV + 2))
            b = job(JV)
            pe.wait_ge(cb_ready, 1)
            pe.transpose(b[:, 0:NV * KT], vrows[:, :], ident[0:NV * KT, 0:NV * KT])
            pe.transpose(b[:, NV * KT:NV * KT + CC], cb_f[:, :], ident[0:CC, 0:CC]).then_inc(job_done, 1)
            pe.wait_ge(s_ctx, 16)
            for n in range(2):
                b = job(JCTX + n)
                for kk in range(2):
                    for bb in range(B):
                        k = 2 * n + kk
                        last = pe.transpose(b[:, kk * BJ + bb * J:kk * BJ + (bb + 1) * J],
                                            ctx_sb[:, bb, k * P:(k + 1) * P], ident[0:J, 0:J])
                last.then_inc(job_done, 1)
            pe.wait_ge(s_wq, 16)
            for k in range(KT):
                turn_weight(JWQ, w_in_sb, 0, k)
            pe.wait_ge(s_wkv, 16)
            for k in range(KT):
                turn_weight(JWK, w_in_sb, KT, k)
            taken(pe, JWQ + 3)
            taken(pe, JWQ + 2)
            taken(pe, JV)
            b = job(JQB)
            for m in range(KT):
                for k in range(KT):
                    last = pe.matmul(b[:, m:m + 1], wT[:, 0, k, m * P:(m + 1) * P], vcol(V_BETA, k),
                                     start=k == 0, stop=k == KT - 1)
            last.then_inc(job_done, 1)
            taken(pe, JWK + 3)
            taken(pe, JWK + 2)
            taken(pe, JCTX)
            taken(pe, JCTX + 1)
            for m in range(KT):
                product(JK + m, [(wT[:, 1, k, m * P:(m + 1) * P], ctxT0[:, k, :]) for k in range(KT)], (P, BJ))
            for k in range(KT):
                turn_weight(JWV, w_in_sb, 2 * KT, k)
            taken(pe, JWV + 3)
            taken(pe, JWV + 2)
            for bb in range(B):
                product(JVV + bb, [(ctxT0[:, k, bb * J:(bb + 1) * J], wT[:, 0, k, :]) for k in range(KT)]
                        + [(ones[0:1, 0:J], bv_row[:, :])], (J, D))
            pe.wait_ge(s_w1, 16 * 5)
            for k in range(KT):
                turn_weight(JWO, w_out_sb, 0, k)
            for k in range(KT):
                turn_weight(JWQ1, wq1_sb, 0, k)
            for m in range(KT):
                product(JK1 + m, [(wk1_sb[:, k, m * P:(m + 1) * P], ctxT0[:, k, :]) for k in range(KT)], (P, BJ))
            for m in range(KT):
                product(JV1 + m, [(wv1_sb[:, k, m * P:(m + 1) * P], ctxT0[:, k, :]) for k in range(KT)], (P, BJ))
            taken(pe, JK1 + 3)
            taken(pe, JK1 + 2)
            for m in range(KT):
                product(JM + m, [(wT[:, 1, k, m * P:(m + 1) * P], k1T[:, k, :]) for k in range(KT)], (P, BJ))
            taken(pe, JM + 3)
            taken(pe, JM + 2)

            def mf(k):
                return m_f[:, k, :, :].rearrange("p b j -> p (b j)")

            for m in range(KT):
                product(JW2 + m, [(w_out_sb[:, k, m * P:(m + 1) * P], mf(k)) for k in range(KT)], (P, BJ))
            product(JCOL, [(ones[:, :], mf(k)) for k in range(KT)], (P, BJ))
            pe.wait_ge(rep_ready, 2 * KT)
            product(JC, [(rep[:, 0, k, :], mf(k)) for k in range(KT)]
                    + [(rep[:, 1, k, :], k1T[:, k, :]) for k in range(KT)], (P, BJ))
            taken(pe, JV1 + 3)
            taken(pe, JV1 + 2)
            for bb in range(B):
                product(JVW + bb, [(v1T[:, k, bb * J:(bb + 1) * J], wo1_sb[:, k, :]) for k in range(KT)], (J, D))
            pe.wait_ge(pick_ready, CC)
            b = job(JP)
            for c in range(CC):
                last = pe.matmul(b[:, 0:1], pick[:, c, :], cb_c[:, c:c + 1], start=c == 0, stop=c == CC - 1)
            last.then_inc(job_done, 1)
            for n in range(NJ - 8, NJ):
                taken(pe, n)
            pe.wait_ge(s_kstack, 16 * 3 * HPT * B)
            pe.wait_ge(s_bias1, 16 * 2 * B)
            pe.wait_ge(act_prepared, 1)
            pe.wait_ge(dve_prepared, 1)

            def turn_z(t, sub):
                pe.wait_ge(z_ready, at(t, SUB, sub + 1))
                if sub == 1:
                    pe.wait_ge(zhi_ready, at(t, SUB, sub))
                    pe.wait_ge(zlo_ready, at(t, SUB, sub))
                b = bank[TURN_BANKS[sub]]
                for k in range(KT):
                    last = pe.transpose(b[:, k * P:(k + 1) * P], z[:, sub % 2, k * P:(k + 1) * P], ident[:, :])
                last.then_inc(z_turned, 1)

            def split3(o, lhs, rhs, ks, more=0):
                n, total = 0, 3 * len(ks) + more
                for k in ks:
                    for l, r in ((0, 0), (0, 1), (1, 0)):
                        last = pe.matmul(o, lhs(l, k), rhs(r, k), start=n == 0, stop=n == total - 1)
                        n += 1
                return last

            wq = (wqT_hi, wqT_lo)
            wo = (woT_hi, woT_lo)
            zt = (zT_hi, zT_lo)
            aT = (attT_hi, attT_lo)
            qh = (q_hi, q_lo)
            kd = (kdiag_hi, kdiag_lo)
            mm = (m_hi, m_lo)
            w2 = (w2_hi, w2_lo)

            def project_q(t, s, t_prev=None):
                pe.wait_ge(zlo_ready, at(t, SUB, SUB))
                pe.wait_ge(zhi_ready, at(t, SUB, SUB))
                for m in range(KT):
                    if m == 2 and t_prev is not None:
                        pe.wait_ge(rd_ready, at(t_prev, 1, 1))
                    if m == 3:
                        pe.wait_ge(qlo_ready, at(t, KT, 1))
                        pe.wait_ge(qhi_ready, at(t, KT, 1))
                    split3(bank[m % 3][:, :], lambda l, k: wq[l][:, k, m * P:(m + 1) * P],
                           lambda r, k: zt[r][:, k, :], range(KT)).then_inc(q_done, 1)
                pe.wait_ge(qlo_ready, at(t, KT, 2))
                pe.wait_ge(qhi_ready, at(t, KT, 2))
                split3(bank[1][0:J, :], lambda l, k: mm[l][:, k, s, :],
                       lambda r, k: zt[r][:, k, :], range(KT)).then_inc(s1z_done, 1)

            def max_scores(t, s):
                for sub in range(SUB):
                    for g in range(KT):
                        u = sub * KT + g
                        if u < KT:
                            pe.wait_ge(qlo_ready, at(t, KT, 3 if u < 2 else 4))
                            pe.wait_ge(qhi_ready, at(t, KT, 3 if u < 2 else 4))
                            if u == 3:
                                pe.wait_ge(s1z_ready, at(t, 1, 1))
                        else:
                            pe.wait_ge(max_taken, at(t, SUB * KT, u - KT + 1))
                        split3(bank[MAX_BANKS[u % KT]][:, 0:GJ], lambda l, k: qh[l][:, g, sub * P:(sub + 1) * P],
                               lambda r, k: kd[r][:, s, g, :], [0]).then_inc(maxs_done, 1)

            def turn_max(t):
                pe.wait_ge(mx_ready, at(t, 1, 1))
                for sub in range(SUB):
                    last = pe.transpose(bank[1][0:2 * H, sub * P:(sub + 1) * P], mx2[:, sub, :], ident[:, :])
                last.then_inc(mx_turned, 1)

            def scores(t, q, s, h):
                if h == 0:
                    pe.wait_ge(mrows_spread, at(t, 16, 16))
                    pe.wait_ge(onehot_ready, at(q, 1, 1))
                    pe.wait_ge(stack_loaded, at(t, 16 * 3 * HPT, 16 * 3 * HPT))
                before = [e for e in range(h) if SCORE_BANKS[e] == SCORE_BANKS[h]]
                if before:
                    pe.wait_ge(prob_ready, at(t, H, before[-1] + 1))
                b = bank[SCORE_BANKS[h]][0:J, :]
                pe.matmul(b, kstack[:, s, h, :], qstack[:, h, :], start=True, stop=False)
                pe.matmul(b, maskw[:, :], onehot[:, :], start=False, stop=True).then_inc(scores_done, 1)

            def attend(t, s, g):
                pe.wait_ge(prob_ready, at(t, H, (g + 1) * HPT))
                pe.wait_ge(out_ready, at(t, SUB, g + 1))
                for a in range(HPT):
                    h = g * HPT + a
                    pe.matmul(bank[3 + g][a * DH:(a + 1) * DH, :], v0[:, s, h * DH:(h + 1) * DH],
                              prob[:, h % NPROB, :], start=True, stop=True)
                for a in range(HPT):
                    h = g * HPT + a
                    last = pe.matmul(bank[2][a * DH:(a + 1) * DH, :], densel[:, g, :], prob[:, h % NPROB, :],
                                     start=g == 0, stop=g == KT - 1)
                last.then_inc(group_used, 1)

            def second_scores(t, s, more):
                if more:
                    pe.wait_ge(max_taken, at(t + 1, SUB * KT, SUB * KT - 3))
                pe.wait_ge(attlo_ready, at(t, KT, KT))
                pe.wait_ge(atthi_ready, at(t, KT, KT))
                split3(bank[2][0:J, :], lambda l, k: w2[l][:, k, s, :],
                       lambda r, k: aT[r][:, k, :], range(KT)).then_inc(s1a_done, 1)

            def turn_second(t, s, more):
                if more:
                    pe.wait_ge(max_taken, at(t + 1, SUB * KT, SUB * KT - 1))
                pe.wait_ge(s1z_ready, at(t, 1, 1))
                pe.wait_ge(s1a_ready, at(t, 1, 1))
                for sub in range(SUB):
                    pe.transpose(bank[7][:, sub * J:(sub + 1) * J], s1z[:, s, sub * P:(sub + 1) * P], ident[0:J, 0:J])
                for sub in range(SUB):
                    last = pe.transpose(bank[0][:, sub * J:(sub + 1) * J], s1t[0:J, sub * P:(sub + 1) * P],
                                        ident[0:J, 0:J])
                last.then_inc(s1_turned, 1)

            def out_proj(t, sub):
                b = bank[3 + sub]
                if sub == 0:
                    pe.wait_ge(att_ready, at(t, KT, KT))
                n = 0
                for k in range(KT):
                    for l, r in ((0, 0), (0, 1), (1, 0)):
                        pe.matmul(b[:, :], aT[l][:, k, sub * P:(sub + 1) * P], wo[r][:, k, :],
                                  start=n == 0, stop=False)
                        n += 1

            def turn_p1(t):
                pe.wait_ge(p1_ready, at(t, 1, 1))
                for sub in range(SUB):
                    last = pe.transpose(bank[7][0:J + 2, sub * P:(sub + 1) * P], p1[:, sub, :], ident[:, :])
                last.then_inc(p1_turned, 1)

            def second_out(t, s, sub):
                pe.wait_ge(p1T_ready, at(t, 1, 1))
                pe.matmul(bank[3 + sub][:, :], s1t[:, sub * P:(sub + 1) * P], vw1[:, s, :],
                          start=False, stop=True).then_inc(out_done, 1)

            pe.wait_ge(pads_ready, 2)
            for sub in range(SUB):
                turn_z(0, sub)
            project_q(0, 0)
            max_scores(0, 0)
            turn_max(0)

            def tile(t, q, s, more=True):
                n, ns = t + 1, 1 - s
                for h in range(AHEAD):
                    scores(t, q, s, h)
                for g in range(KT):
                    if more and g == KT - 1:
                        turn_z(n, 0)
                    for h in range(g * HPT + AHEAD, min((g + 1) * HPT + AHEAD, H)):
                        scores(t, q, s, h)
                    if more and g == KT - 1:
                        turn_z(n, 1)
                        pe.wait_ge(prob_ready, at(t, H, H - 1))
                        turn_z(n, 2)
                        pe.wait_ge(prob_ready, at(t, H, H))
                        turn_z(n, 3)
                    attend(t, s, g)
                if more:
                    project_q(n, ns, t)
                if more:
                    max_scores(n, ns)
                second_scores(t, s, more)
                if more:
                    turn_max(n)
                out_proj(t, 0)
                turn_second(t, s, more)
                out_proj(t, 1)
                out_proj(t, 2)
                turn_p1(t)
                out_proj(t, 3)
                for sub in range(SUB):
                    second_out(t, s, sub)

            with pe.Fori(0, QT - 1) as i:
                for s in range(2):
                    tile(2 * i + s, i, s)
            tile(NT - 2, QT - 1, 0)
            tile(NT - 1, QT - 1, 1, more=False)

        def takes(n):
            b = bank[n % 8]
            for j0, dst in ((JWQ, wT[:, 0]), (JWK, wT[:, 1]), (JWV, wT[:, 0]), (JWO, wT[:, 0]), (JWQ1, wT[:, 1])):
                if j0 <= n < j0 + KT:
                    return dst[:, n - j0, :], b[:, :], None, None
            if JCTX <= n < JCTX + 2:
                k = 2 * (n - JCTX)
                return ctxT0[:, k:k + 2, :].rearrange("p k j -> p (k j)"), b[:, 0:2 * BJ], None, None
            if JVV <= n < JVV + B:
                return v0[:, n - JVV, :], b[0:J, :], None, None
            if JVW <= n < JVW + B:
                return vw1[0:J, n - JVW, :], b[0:J, :], None, None
            for j0, dst, v, f in ((JK, kT, V_BK, None), (JK1, k1T, V_BK1, None), (JV1, v1T, V_BV1, None),
                                  (JM, m_f, None, SCALE1), (JW2, w2_f, None, None)):
                if j0 <= n < j0 + KT:
                    d = dst[:, n - j0]
                    if len(d.shape) == 3:
                        d = d.rearrange("p b j -> p (b j)")
                    return d, b[:, 0:BJ], None if v is None else vcol(v, n - j0), f
            if n == JCOL:
                return colm[:, :, :].rearrange("p b j -> p (b j)"), b[:, 0:BJ], None, None
            if n == JC:
                return cvec[:, :, :].rearrange("p b j -> p (b j)"), b[:, 0:BJ], None, None
            if n == JP:
                return ce_cs[:, :], b[:, 0:1], None, None

        @block.scalar
        def _(act):
            def take(n):
                act.wait_ge(job_done, n + 1)
                if n == JV:
                    act.activation(cb_c[:, :], bank[0][:, NV * KT:NV * KT + CC], ACT.Copy).then_inc(cb_ready, 1)
                    act.activation(vcols[:, :], bank[0][:, 0:NV * KT], ACT.Copy).then_inc(act_took, 1)
                    return
                dst, src, bias, factor = takes(n)
                if bias is not None:
                    act.wait_ge(act_took, 1)
                    act.activation(dst, src, ACT.Identity, bias=bias).then_inc(act_took, 1)
                else:
                    act.activation(dst, src, ACT.Copy, scale=1.0 if factor is None else factor)\
                       .then_inc(act_took, 1)

            for n in range(JV, JQB, 2):
                take(n)
            act.wait_ge(gs_ready, 1)
            for k in range(KT):
                taken(act, JWQ + k)
                act.activation(wqT_hi[:, k, :], wT[:, 0, k, :], ACT.Copy, scale=gs[:, k:k + 1]).then_inc(hi_done, 1)
            for n in range(JK, JK + KT, 2):
                take(n)
            for n in range(JK, JK + KT):
                taken(act, n)
            act.activation(kT_hi[:, :, :, :], kT[:, :, :, :], ACT.Copy).then_inc(hi_done, 1)
            act.wait_ge(wq_split, KT)
            for n in range(JWV, JWQ1, 2):
                take(n)
            for k in range(KT):
                taken(act, JWO + k)
                act.activation(woT_hi[:, k, :], wT[:, 0, k, :], ACT.Copy).then_inc(hi_done, 1)
            for n in range(JWQ1, JW2, 2):
                take(n)
            for n in range(JM, JM + KT):
                taken(act, n)
            act.activation(m_hi[:, :, :, :], m_f[:, :, :, :], ACT.Copy).then_inc(hi_done, 1)
            for n in range(JW2, JCOL, 2):
                take(n)
            for n in range(JW2, JW2 + KT):
                taken(act, n)
            act.activation(w2_hi[:, :, :, :], w2_f[:, :, :, :], ACT.Copy).then_inc(hi_done, 1)
            for n in range(JCOL, NJ - 1, 2):
                take(n)
            take(JP)
            act.wait_ge(act_took, NJ // 2 + 1)
            act.wait_ge(hi_done, 2 * KT + 3)
            act.activation(ce_cs2[:, :], ce_cs[:, :], ACT.Copy).then_inc(act_prepared, 1)

            def z_high(t, sub):
                act.wait_ge(z_turned, at(t, SUB, sub + 1))
                act.activation(zT_hi[:, :, sub * P:(sub + 1) * P],
                               bank[TURN_BANKS[sub]][:, :].rearrange("p (k c) -> p k c", k=KT), ACT.Copy).then_inc(zhi_ready, 1)

            def q_high(t, s, before=None):
                for m in range(KT):
                    if before is not None and m >= 2:
                        att_high(before, m - 2)
                    act.wait_ge(q_done, at(t, KT, m + 1))
                    act.activation(q_hi[:, m, :], bank[m % 3][:, :], ACT.Identity,
                                   bias=q_bias[:, m:m + 1]).then_inc(qhi_ready, 1)
                act.wait_ge(s1z_done, at(t, 1, 1))
                act.activation(s1z[:, s, :], bank[1][0:J, :], ACT.Copy).then_inc(s1z_ready, 1)

            def max_rows(t):
                act.wait_ge(mx_turned, at(t, 1, 1))
                act.activation(mrows, bank[1][0:2 * H, :], ACT.Copy).then_inc(mrows_ready, 1)

            def att_high(t, g):
                act.wait_ge(att_ready, at(t, KT, g + 1))
                act.activation(attT_hi[:, g, :], att[:, g % 2, :], ACT.Copy).then_inc(atthi_ready, 1)

            for sub in range(SUB):
                z_high(0, sub)
            q_high(0, 0)
            max_rows(0)

            def tile(t, s, more=True):
                n, ns = t + 1, 1 - s
                for h in range(H):
                    act.wait_ge(scores_done, at(t, H, h + 1))
                    if h >= NPROB:
                        act.wait_ge(group_used, at(t, KT, (h - NPROB) // HPT + 1))
                    act.activation(prob[:, h % NPROB, :], bank[SCORE_BANKS[h]][0:J, :], ACT.Exp).then_inc(prob_ready, 1)
                    if more and h == H - 3:
                        z_high(n, 0)
                if more:
                    for sub in range(1, SUB):
                        z_high(n, sub)
                    q_high(n, ns, before=t)
                else:
                    att_high(t, 0)
                    att_high(t, 1)
                att_high(t, 2)
                att_high(t, 3)
                act.wait_ge(s1a_done, at(t, 1, 1))
                act.activation(s1t[0:J, :], bank[2][0:J, :], ACT.Copy).then_inc(s1a_ready, 1)
                if more:
                    max_rows(n)
                act.wait_ge(nmax1_ready, at(t, 1, 1))
                for sub in range(SUB):
                    act.activation(e1[:, sub, :], p1[:, sub, 0:J], ACT.Exp, bias=nmax1[:, sub:sub + 1],
                                   accum_out=sum1[:, sub:sub + 1]).then_inc(e1_ready, 1)
                act.wait_ge(p1_turned, at(t, 1, 1))
                act.activation(s1t[:, :], bank[7][0:J + 2, :], ACT.Copy).then_inc(p1T_ready, 1)

            with act.Fori(0, QT - 1) as i:
                for s in range(2):
                    tile(2 * i + s, s)
            tile(NT - 2, 0)
            tile(NT - 1, 1, more=False)

        @block.vector
        def _(dve):
            nprep = 0

            def link(ins):
                nonlocal nprep
                nprep += 1
                ins.then_inc(prep_step, 1)
                dve.wait_ge(prep_step, nprep)

            def take(n):
                dve.wait_ge(job_done, n + 1)
                if n == JQB:
                    link(dve.tensor_tensor(q_bias[:, :], bank[n % 8][:, 0:KT],
                                           vcols[:, V_BQ * KT:(V_BQ + 1) * KT], ALU.add))
                    dve.tensor_scalar(q_bias[:, :], q_bias[:, :], SCALE0, None, ALU.mult).then_inc(dve_took, 1)
                    return
                dst, src, bias, factor = takes(n)
                if bias is not None:
                    dve.tensor_scalar(dst, src, bias, None, ALU.add).then_inc(dve_took, 1)
                elif factor is not None:
                    dve.tensor_scalar(dst, src, factor, None, ALU.mult).then_inc(dve_took, 1)
                else:
                    dve.tensor_copy(dst, src).then_inc(dve_took, 1)

            dve.wait_ge(s_vec, 16 * (NV + 2))
            dve.tensor_scalar(cb_f[:, :], cb_i[:, :], 0, J, ALU.max, ALU.min).then_inc(cb_ready, 1)
            for n in range(JV + 1, JQB, 2):
                take(n)
            taken(dve, JV)
            dve.tensor_scalar(gs[:, :], vcols[:, V_GAMMA * KT:(V_GAMMA + 1) * KT], SCALE0, None,
                              ALU.mult).then_inc(gs_ready, 1)
            dve.wait_ge(gs_ready, 1)
            for k in range(KT):
                dve.wait_ge(hi_done, k + 1)
                dve.scalar_tensor_tensor(out=wqT_lo[:, k, :], in0=wT[:, 0, k, :], scalar=gs[:, k:k + 1],
                                         in1=wqT_hi[:, k, :], op0=ALU.mult, op1=ALU.subtract).then_inc(wq_split, 1)
            take(JQB)
            for n in range(JK + 1, JK + KT, 2):
                take(n)
            dve.wait_ge(hi_done, KT + 1)
            dve.tensor_tensor(kT_lo[:, :, :, :], kT[:, :, :, :], kT_hi[:, :, :, :], ALU.subtract).then_inc(k_split, 1)
            for n in range(JWV + 1, JWQ1, 2):
                take(n)
            for k in range(KT):
                dve.wait_ge(hi_done, KT + 2 + k)
                dve.tensor_tensor(woT_lo[:, k, :], wT[:, 0, k, :], woT_hi[:, k, :],
                                  ALU.subtract).then_inc(wo_split, 1)
            for n in range(JWQ1 + 1, JM, 2):
                take(n)
            dve.wait_ge(const_ready, NCONST)
            for k in range(KT):
                dve.tensor_scalar(rep[:, 0, k, :], ones[:, :], vcol(V_BOUT, k), None, ALU.mult)\
                   .then_inc(rep_ready, 1)
                dve.tensor_scalar(rep[:, 1, k, :], ones[:, :], vcol(V_BQ1, k), SCALE1, ALU.mult, ALU.mult)\
                   .then_inc(rep_ready, 1)
            for n in range(JM + 1, JW2, 2):
                take(n)
            dve.wait_ge(hi_done, 2 * KT + 2)
            dve.tensor_tensor(m_lo[:, :, :, :], m_f[:, :, :, :], m_hi[:, :, :, :], ALU.subtract).then_inc(prep_lo, 1)
            dve.wait_ge(s_word, 16 * 7)
            link(dve.tensor_copy(wb32[:, :], wb_i[:, :]))
            dve.tensor_copy(widx[:, 0:W], wb32[:, 0:W])
            link(dve.tensor_scalar(widx[:, W:2 * W], wb32[:, 1:W + 1], 1.0, None, ALU.subtract))
            link(dve.tensor_scalar(widx2[:, :], widx[:, :], 0.0, float(NCB), ALU.is_lt, ALU.mult))
            link(dve.tensor_tensor(widx2[:, :], widx2[:, :], widx[:, :], ALU.add))
            link(dve.tensor_scalar(widx[:, :], widx2[:, :], 0.0, float(NCB - 1), ALU.max, ALU.min))
            for c in range(CC):
                dve.tensor_scalar(pick[:, c, :], widx[:, :], kcol[:, c:c + 1], None, ALU.is_equal)\
                   .then_inc(pick_ready, 1)
            for n in range(JW2 + 1, JCOL, 2):
                take(n)
            dve.wait_ge(hi_done, 2 * KT + 3)
            dve.tensor_tensor(w2_lo[:, :, :, :], w2_f[:, :, :, :], w2_hi[:, :, :, :], ALU.subtract).then_inc(prep_lo, 1)
            take(JC)
            take(JVW + 1)
            dve.wait_ge(k_split, 1)
            for b in range(B):
                for a in range(HPT):
                    rows = slice(DH * a, DH * (a + 1))
                    for dst, src in ((kdiag_hi, kT_hi), (kdiag_lo, kT_lo)):
                        dve.tensor_copy(dst[rows, b, :, a * J:(a + 1) * J], src[rows, :, b, :]).then_inc(prep_lo, 1)
            link(dve.tensor_copy(wcol[:, :], wcol_i[:, :]))
            taken(dve, JP)
            link(dve.tensor_copy(cend[:, :], ce_cs[W:2 * W, :]))
            link(dve.tensor_copy(wlo[:, :], wcol[:, 0:1]))
            link(dve.tensor_copy(whi[:, :], wcol[:, 1:2]))
            bounds = ((ce_cs[0:W, :], cend[:, :]), (wcol[:, 2:3], wcol[:, 0:1]), (wcol[:, 1:2], wcol[:, 3:4]))
            for r, (lo, hi) in enumerate(bounds):
                link(dve.tensor_scalar(ge[:, r, :], tok[:, 0:J], lo, None, ALU.is_ge))
                link(dve.scalar_tensor_tensor(out=rng[:, r, :], in0=tok[:, 0:J], scalar=hi, in1=ge[:, r, :],
                                              op0=ALU.is_lt, op1=ALU.mult))
            link(dve.tensor_tensor(rng[:, 0, :], rng[:, 0, :], rng[:, 1, :], ALU.max))
            link(dve.tensor_tensor(rng[:, 0, :], rng[:, 0, :], rng[:, 2, :], ALU.max))
            dve.tensor_copy(maskw[0:W, :], rng[:, 0, :]).then_inc(prep_lo, 1)
            for b in range(B):
                dve.tensor_copy(kstack[96:P, b, :, :], msel[96:P, :, :]).then_inc(prep_lo, 1)
            dve.wait_ge(prep_lo, 2 + 2 * B * HPT + 1 + B)
            dve.wait_ge(wo_split, KT)
            dve.wait_ge(dve_took, NJ // 2)
            dve.memset(p1ones[:, :], 1.0).then_inc(out_ready, SUB)
            dve.wait_ge(out_ready, SUB)
            dve.tensor_copy(dve_mark[:, :], p1ones[:, 0:1]).then_inc(dve_prepared, 1)

            cnt = [0]
            base = [0]

            def count(ins):
                cnt[0] += 1
                ins.then_inc(step, 1)

            def own(ins):
                count(ins)
                dve.wait_ge(step, base[0] + cnt[0])

            def normalise(t, q, s):
                for sub in range(SUB):
                    dve.wait_ge(x_loaded[s][sub], at(q, 16, 16))
                    ins = dve.bn_stats(stats[:, sub, :], xs[s][:, sub, :])
                    if sub < SUB - 1:
                        count(ins)
                own(ins)
                even, odd = stats[:, :, 0:3], stats[:, :, 3:6]
                count(dve.tensor_tensor(mean[s][:, :], even[:, :, 1], odd[:, :, 1], ALU.add))
                count(dve.tensor_tensor(mdiff[:, :], even[:, :, 1], odd[:, :, 1], ALU.subtract))
                own(dve.tensor_tensor(veps[:, :], even[:, :, 2], odd[:, :, 2], ALU.add))
                count(dve.tensor_scalar(mean[s][:, :], mean[s][:, :], 0.5, None, ALU.mult))
                count(dve.tensor_tensor(mdiff[:, :], mdiff[:, :], mdiff[:, :], ALU.mult))
                own(dve.tensor_scalar(veps[:, :], veps[:, :], 1.0 / D, EPS, ALU.mult, ALU.add))
                dve.scalar_tensor_tensor(out=veps[:, :], in0=mdiff[:, :], scalar=0.25, in1=veps[:, :],
                                         op0=ALU.mult, op1=ALU.add).then_inc(veps_ready, 1)
                dve.wait_ge(rstd_ready, at(t, 1, 1))
                own(dve.reciprocal(std[s][:, :], rstd[:, :]))

            def z_part(t, s, sub):
                if sub >= 2:
                    dve.wait_ge(z_turned, at(t, SUB, sub - 1))
                dve.tensor_scalar(z[:, sub % 2, :], xs[s][:, sub, :], mean[s][:, sub:sub + 1], rstd[:, sub:sub + 1],
                                  ALU.subtract, ALU.mult).then_inc(z_ready, 1)

            def z_low(t, sub):
                dve.wait_ge(zhi_ready, at(t, SUB, sub + 1))
                part = slice(sub * P, (sub + 1) * P)
                dve.tensor_tensor(zT_lo[:, :, part], bank[TURN_BANKS[sub]][:, :].rearrange("p (k c) -> p k c", k=KT),
                                  zT_hi[:, :, part], ALU.subtract).then_inc(zlo_ready, 1)

            def q_low(t, m):
                dve.wait_ge(qhi_ready, at(t, KT, m + 1))
                dve.scalar_tensor_tensor(out=q_lo[:, m, :], in0=bank[m % 3][:, :], scalar=q_bias[:, m:m + 1],
                                         in1=q_hi[:, m, :], op0=ALU.add, op1=ALU.subtract).then_inc(qlo_ready, 1)

            def take_max(t, us=range(SUB * KT)):
                for u in us:
                    sub, g = u // KT, u % KT
                    dve.wait_ge(maxs_done, at(t, SUB * KT, u + 1))
                    dve.tensor_reduce(mx[:, sub, g * HPT:(g + 1) * HPT],
                                      bank[MAX_BANKS[u % KT]][:, 0:GJ].rearrange("p (a j) -> p a j", a=HPT), AX.X,
                                      ALU.max).then_inc(max_taken, 1)

            def split_max(t):
                dve.wait_ge(max_taken, at(t, SUB * KT, SUB * KT))
                own(dve.tensor_copy(mx_hr[:, :, :], mx[:, :, :]))
                own(dve.tensor_copy(mx2[:, :, 0:H], mx_hr[:, :, :]))
                dve.tensor_tensor(mx2[:, :, H:2 * H], mx[:, :, :], mx_hr[:, :, :], ALU.subtract).then_inc(mx_ready, 1)

            def one_hot():
                own(dve.tensor_scalar(att[0:W, 0, :], tok[:, :], wlo[:, :], None, ALU.is_ge))
                dve.scalar_tensor_tensor(out=onehot[0:W, :], in0=tok[:, :], scalar=whi[:, :], in1=att[0:W, 0, :],
                                         op0=ALU.is_lt, op1=ALU.mult).then_inc(onehot_ready, 1)

            def invert(t):
                dve.wait_ge(group_used, at(t, KT, KT))
                dve.reciprocal(rd, bank[2][:, :]).then_inc(rd_ready, 1)

            def divide(t, g):
                own(dve.stream_shuffle(att[:, g % 2, :], rd, [g] * DH))
                dve.tensor_tensor(att[:, g % 2, :], bank[3 + g][:, :], att[:, g % 2, :], ALU.mult).then_inc(att_ready, 1)

            def att_low(t, g):
                dve.wait_ge(atthi_ready, at(t, KT, g + 1))
                dve.tensor_tensor(attT_lo[:, g, :], att[:, g % 2, :], attT_hi[:, g, :],
                                  ALU.subtract).then_inc(attlo_ready, 1)

            normalise(0, 0, 0)
            z_part(0, 0, 0)
            z_part(0, 0, 1)
            z_part(0, 0, 2)
            z_low(0, 0)
            z_part(0, 0, 3)
            z_low(0, 1)
            z_low(0, 2)
            z_low(0, 3)
            for m in range(KT):
                q_low(0, m)
            one_hot()
            take_max(0)
            split_max(0)
            own(dve.memset(p1[:, :, J:J + 2], 1.0))
            first = cnt[0]
            NSTEP = 2 * (SUB + 6 + 1 + 2 * SUB + 1 + SUB + 2 + KT) + 3

            def tile(t, q, s, more=True):
                n, ns, nq = t + 1, 1 - s, q + s
                if more:
                    normalise(n, nq, ns)
                    z_part(n, ns, 0)
                    z_part(n, ns, 1)
                    z_part(n, ns, 2)
                    z_low(n, 0)
                    z_part(n, ns, 3)
                    z_low(n, 1)
                    z_low(n, 2)
                    z_low(n, 3)
                invert(t)
                for g in range(KT):
                    if g == 0:
                        dve.wait_ge(rd_ready, at(t, 1, 1))
                    if g >= 2:
                        att_low(t, g - 2)
                        dve.wait_ge(attlo_ready, at(t, KT, g - 1))
                    if more:
                        q_low(n, g)
                    divide(t, g)
                if more:
                    take_max(n, range(KT))
                att_low(t, KT - 2)
                if more:
                    take_max(n, range(KT, 2 * KT))
                att_low(t, KT - 1)
                if more:
                    take_max(n, range(2 * KT, SUB * KT))
                    split_max(n)
                for sub in range(SUB):
                    own(dve.scalar_tensor_tensor(out=sc1b[:, sub, :], in0=colm[:, s, :], scalar=mean[s][:, sub:sub + 1],
                                                 in1=cvec[:, s, :], op0=ALU.mult, op1=ALU.add))
                dve.wait_ge(s1_turned, at(t, 1, 1))
                for sub in range(SUB):
                    own(dve.scalar_tensor_tensor(out=sc1b[:, sub, :], in0=bank[7][:, sub * J:(sub + 1) * J],
                                                 scalar=std[s][:, sub:sub + 1], in1=sc1b[:, sub, :],
                                                 op0=ALU.mult, op1=ALU.add))
                own(dve.tensor_tensor(sc1, sc1b[:, :, :],
                                      bank[0][:, 0:SUB * J].rearrange("p (s j) -> p s j", s=SUB), ALU.add))
                dve.tensor_reduce(nmax1[:, :], sc1, AX.X, ALU.max, negate=True).then_inc(nmax1_ready, 1)
                dve.wait_ge(e1_ready, at(t, SUB, SUB))
                own(dve.reciprocal(rsum1[:, :], sum1[:, :]))
                for sub in range(SUB):
                    ins = dve.tensor_scalar(p1[:, sub, 0:J], e1[:, sub, :], rsum1[:, sub:sub + 1], None, ALU.mult)
                    if sub < SUB - 1:
                        own(ins)
                    else:
                        ins.then_inc(p1_ready, 1)
                if more and s == 1:
                    own(dve.tensor_scalar(wlo[:, :], wlo[:, :], float(T), None, ALU.subtract))
                    own(dve.tensor_scalar(whi[:, :], whi[:, :], float(T), None, ALU.subtract))
                    one_hot()
                for sub in range(SUB):
                    dve.wait_ge(out_done, at(t, SUB, sub + 1))
                    dve.tensor_tensor(xs[s][:, sub, :], bank[3 + sub][:, :], xs[s][:, sub, :],
                                      ALU.add).then_inc(out_ready, 1)

            with dve.Fori(0, QT - 1) as i:
                base[0] = i * NSTEP + first
                cnt[0] = 0
                for s in range(2):
                    tile(2 * i + s, i, s)
                assert cnt[0] == NSTEP, cnt[0]
            base[0] = (QT - 1) * NSTEP + first
            cnt[0] = 0
            tile(NT - 2, QT - 1, 0)
            tile(NT - 1, QT - 1, 1, more=False)


_INS = ["x", "ctx_1024", "itok_S_0_4092", "L0_xattn_word_boundaries", "L0_xattn_ln_gamma", "L0_xattn_ln_beta",
        "L0_xattn_in_proj_w", "L0_xattn_in_proj_b", "L0_xattn_out_w", "L0_xattn_out_b",
        "L1_xattn_Wq", "L1_xattn_bq", "L1_xattn_Wk", "L1_xattn_bk", "L1_xattn_Wv", "L1_xattn_bv",
        "L1_xattn_Wo", "L1_xattn_bo"]


def kernel(**inputs):
    import numpy as _np
    import concourse.bacc as _bacc
    from concourse import mybir as _mybir
    from concourse.bass_utils import run_bass_kernel_spmd as _run

    nc = _bacc.Bacc("TRN2", target_bir_lowering=False, num_devices=1)
    arrays, args = {}, []
    for name in _INS:
        a = _np.ascontiguousarray(inputs[name])
        arrays[f"in_{name}_dram"] = a
        args.append(nc.dram_tensor(f"in_{name}_dram", a.shape, _mybir.dt.from_np(a.dtype), kind="ExternalInput").ap())
    shape = tuple(inputs["x"].shape)
    args.append(nc.dram_tensor("out_0_dram", shape, _mybir.dt.float32, kind="ExternalOutput").ap())
    two_cross_attentions(nc, *args)
    r = _run(nc, [arrays], core_ids=[0])
    return r.results[0]["out_0_dram"]
```

```python
from contextlib import ExitStack

import concourse.bass as bass
from concourse import mybir

ALU = mybir.AluOpType
ACT = mybir.ActivationFunctionType
AX = mybir.AxisListType
F32 = mybir.dt.float32
F32R = mybir.dt.float32r
F16 = mybir.dt.float16
BF16 = mybir.dt.bfloat16
I32 = mybir.dt.int32

P = 128
EPS = 1e-5


def two_cross_attentions(
    nc: bass.Bass,
    x: bass.AP,
    ctx_in: bass.AP,
    char_bounds: bass.AP,
    word_bounds: bass.AP,
    gamma: bass.AP,
    beta: bass.AP,
    w_in: bass.AP,
    b_in: bass.AP,
    w_out: bass.AP,
    b_out: bass.AP,
    wq1: bass.AP,
    bq1: bass.AP,
    wk1: bass.AP,
    bk1: bass.AP,
    wv1: bass.AP,
    bv1: bass.AP,
    wo1: bass.AP,
    bo1: bass.AP,
    out: bass.AP,
):
    B, S, D = x.shape
    J = ctx_in.shape[1]
    H = 16
    DH = D // H
    KT = D // P
    HPT = P // DH
    W = word_bounds.shape[0] - 1
    T = 512
    SUB = T // P
    QT = S // T
    NT = B * QT
    NCB = char_bounds.shape[0]
    CC = NCB // P
    SCALE0 = float(DH) ** -0.5
    SCALE1 = float(D // 8) ** -0.5
    GJ = HPT * J
    BJ = B * J
    NV = 9
    AHEAD = 2
    NPROB = HPT + AHEAD
    assert B == 2 and D == 512 and J <= 77 and W == 64 and CC == 16 and DH == 32

    x_t = x.rearrange("b (q s p) d -> b q p s d", s=SUB, p=P)
    out_t = out.rearrange("b (q s p) d -> b q p s d", s=SUB, p=P)

    with ExitStack() as ctx:
        def sem(name):
            return ctx.enter_context(nc.semaphore(name))

        def keep(name, shape, dt):
            return ctx.enter_context(nc.sbuf_tensor(name, shape, dt))

        wqT_hi = keep("wqT_hi", [P, KT, D], F32R)
        wqT_lo = keep("wqT_lo", [P, KT, D], F32R)
        woT_hi = keep("woT_hi", [P, KT, D], F32R)
        woT_lo = keep("woT_lo", [P, KT, D], F32R)
        kdiag_hi = keep("kdiag_hi", [P, B, KT, GJ], F32R)
        kdiag_lo = keep("kdiag_lo", [P, B, KT, GJ], F32R)
        kstack = keep("kstack", [P, B, H, J], F32R)
        maskw = keep("maskw", [P, J], F32R)
        densel = keep("densel", [J, KT + 1, DH], F32)
        v0 = keep("v0", [J, B, D], F32)
        vw1_hi = keep("vw1_hi", [J + 2, B, D], F32R)
        vw1_lo = keep("vw1_lo", [J + 2, B, D], F32R)
        m_hi = keep("m_hi", [P, KT, B, J], F32R)
        m_lo = keep("m_lo", [P, KT, B, J], F32R)
        w2_hi = keep("w2_hi", [P, KT, B, J], F32R)
        w2_lo = keep("w2_lo", [P, KT, B, J], F32R)
        colm = keep("colm", [P, B, J], F32)
        c_col = keep("c_col", [J, B], F32)
        ident = keep("ident", [P, P], F32)
        q_bias = keep("q_bias", [P, KT], F32)
        bv_cols = keep("bv_cols", [P, KT], F32)
        tok = keep("tok", [W, T], F16)
        wlo = keep("wlo", [W, 1], F32)
        whi = keep("whi", [W, 1], F32)

        banks = ctx.enter_context(nc.psum_tensor("banks", [P, 8, 512], F32))
        bank = [banks[:, i, :] for i in range(8)]

        xs = [keep(f"x{i}", [P, SUB, D], F32) for i in range(2)]
        att = keep("att", [P, 2, T], F32)
        stats = keep("stats", [P, SUB, 6], F32)
        mean = [keep(f"mean{i}", [P, SUB], F32) for i in range(2)]
        mdiff = keep("mdiff", [P, SUB], F32)
        veps = keep("veps", [P, SUB], F32)
        mhalf = keep("mhalf", [P, SUB], F32)
        rstd = keep("rstd", [P, SUB], F32)
        std = [keep(f"std{i}", [P, SUB], F32) for i in range(2)]

        with ExitStack() as prep:
            def tmp(name, shape, dt):
                return prep.enter_context(nc.sbuf_tensor(name, shape, dt))

            ones = tmp("ones", [P, P], F32)
            vcols = tmp("vcols", [P, NV * KT], F32)
            w_in_sb = tmp("w_in_sb", [P, 3 * KT, D], F32)
            wo1_sb = w_in_sb[:, 0:KT, :]
            wk1_sb = w_in_sb[:, KT:2 * KT, :]
            w_out_sb = tmp("w_out_sb", [P, KT, D], F32)
            wq1_sb = tmp("wq1_sb", [P, KT, D], F32)
            wv1_sb = tmp("wv1_sb", [P, KT, D], F32)
            wT1 = tmp("wT1", [P, KT, D], F32)
            vw1 = wT1[0:J + 2, 0:B, :]
            with ExitStack() as early:
                ctx_sb = early.enter_context(nc.sbuf_tensor("ctx_sb", [J, B, D], F32))
            pick = tmp("pick", [P, CC, 2 * W], BF16)
            bq1_cols = tmp("bq1_cols", [P, KT], F32)
            kT = tmp("kT", [P, KT, B, J], F32)
            kT_hi = tmp("kT_hi", [P, KT, B, J], F32R)
            kT_lo = tmp("kT_lo", [P, KT, B, J], F32R)
            vwT = kT[:, :, :, :].rearrange("p k b j -> p k (b j)")
            k1T = tmp("k1T", [P, KT, BJ], F32)
            m_f = tmp("m_f", [P, KT, B, J], F32)
            v1T = tmp("v1T", [P, KT, BJ], F32)
            w2_f = tmp("w2_f", [P, KT, B, J], F32)
            vrows = tmp("vrows", [NV * KT, P], F32)
            gs = tmp("gs", [P, KT], F32)
            cb_i = tmp("cb_i", [CC, P], I32)
            cb_f = tmp("cb_f", [CC, P], F32)
            cb_c = tmp("cb_c", [P, CC], BF16)
            wb_i = tmp("wb_i", [P, W + 1], I32)
            wb32 = tmp("wb32", [P, W + 1], F32)
            widx = tmp("widx", [P, 2 * W], F32)
            widx2 = tmp("widx2", [P, 2 * W], F32)
            kcol = tmp("kcol", [P, CC], F32)
            wcol_i = tmp("wcol_i", [W, 4], I32)
            wcol = tmp("wcol", [W, 4], F32)
            ce_cs = tmp("ce_cs", [P, 1], F32)
            act_mark = tmp("act_mark", [P, 1], F32)
            beta_rows = tmp("beta_rows", [P, D], F32)
            p1ones = tmp("p1ones", [P, 2], F32)
            dve_mark = tmp("dve_mark", [P, 1], F32)
            cend = tmp("cend", [W, 1], F32)
            ge = tmp("ge", [W, 3, J], F32)
            rng = tmp("rng", [W, 3, J], F32)
            wT0 = tmp("wT0", [P, KT, D], F32)
            ctxT0 = tmp("ctxT0", [P, KT, BJ], F32)
            v0T = tmp("v0T", [P, KT, BJ], F32)

        with ExitStack() as last_only:
            rd_last = last_only.enter_context(nc.sbuf_tensor("rd_last", [P, 2, T], F32))
        zT_hi = keep("zT_hi", [P, KT, T], F32R)
        zT_lo = keep("zT_lo", [P, KT, T], F32R)
        q_hi = keep("q_hi", [P, KT, T], F32R)
        q_lo = keep("q_lo", [P, KT, T], F32R)
        qstack = keep("qstack", [P, H, T], F32R)
        onehot = keep("onehot", [P, T], F32R)
        with ExitStack() as heads_only:
            prob = heads_only.enter_context(nc.sbuf_tensor("prob", [J, NPROB, T], F32))
        assert NPROB == 6
        begun = keep("begun", [W, T], F32)
        rd = keep("rd", [P, T], F32)
        s1t = keep("s1t", [J, T], F32)
        p1T_hi = keep("p1T_hi", [J + 2, T], F32R)
        p1T_lo = keep("p1T_lo", [J + 2, T], F32R)
        mrows = keep("mrows", [2 * H, T], F32)
        s1z = keep("s1z", [J, 2, T], F32)
        attT_hi = keep("attT_hi", [P, KT, T], F32R)
        with ExitStack() as z_only:
            z = z_only.enter_context(nc.sbuf_tensor("z", [P, SUB, D], F32))
        attT_lo = keep("attT_lo", [P, KT, T], F32R)
        p1 = keep("p1", [P, SUB, J + 2], F32)
        sc1 = p1[:, :, 0:J]
        sc1b = keep("sc1b", [P, SUB, J], F32)
        mx = sc1b[:, :, 0:H]
        mx_hr = sc1b[:, :, H:2 * H].bitcast(F32R)
        mx2 = keep("mx2", [P, SUB, 2 * H], F32)
        nmax1 = keep("nmax1", [P, SUB], F32)
        sum1 = keep("sum1", [P, SUB], F32)
        rsum1 = keep("rsum1", [P, SUB], F32)
        e1 = sc1b

        s_vec = sem("s_vec")
        s_word = sem("s_word")
        s_ctx = sem("s_ctx")
        s_wq = sem("s_wq")
        s_wk = sem("s_wk")
        s_wv = sem("s_wv")
        s_w1 = [sem(f"s_w1_{i}") for i in range(5)]
        s_bias1 = sem("s_bias1")
        s_kstack = sem("s_kstack")
        const_ready = sem("const_ready")
        job_done = sem("job_done")
        act_took = sem("act_took")
        dve_took = sem("dve_took")
        pool_step = sem("pool_step")
        cb_ready = sem("cb_ready")
        gs_ready = sem("gs_ready")
        hi_done = sem("hi_done")
        wo_split = sem("wo_split")
        prep_lo = sem("prep_lo")
        qb_product = sem("qb_product")
        qb_summed = sem("qb_summed")
        wq_split = sem("wq_split")
        k_split = sem("k_split")
        kdiag_done = sem("kdiag_done")
        v0T_done = sem("v0T_done")
        v0T_ready = sem("v0T_ready")
        v0_done = sem("v0_done")
        v0_ready = sem("v0_ready")
        prep_step = sem("prep_step")
        bq1_ready = sem("bq1_ready")
        pick_ready = sem("pick_ready")
        act_prepared = sem("act_prepared")
        dve_prepared = sem("dve_prepared")
        x_loaded = [[sem(f"x_loaded{i}_{sub}") for sub in range(SUB)] for i in range(2)]
        x_stored = [sem(f"x_stored{sub}") for sub in range(SUB)]
        stack_loaded = sem("stack_loaded")
        step = sem("step")
        veps_ready = sem("veps_ready")
        rstd_ready = sem("rstd_ready")
        z_ready = sem("z_ready")
        z_turned = sem("z_turned")
        zhi_ready = sem("zhi_ready")
        zlo_ready = sem("zlo_ready")
        q_done = sem("q_done")
        qhi_ready = sem("qhi_ready")
        qlo_ready = sem("qlo_ready")
        s1z_done = sem("s1z_done")
        s1z_ready = sem("s1z_ready")
        maxs_done = sem("maxs_done")
        max_taken = sem("max_taken")
        mx_ready = sem("mx_ready")
        mx_turned = sem("mx_turned")
        mrows_ready = sem("mrows_ready")
        mrows_spread = [sem(f"mrows_spread{i}") for i in range(2)]
        pads_ready = sem("pads_ready")
        rd_ready = sem("rd_ready")
        onehot_ready = sem("onehot_ready")
        scores_done = sem("scores_done")
        prob_ready = sem("prob_ready")
        group_used = sem("group_used")
        att_ready = sem("att_ready")
        atthi_ready = sem("atthi_ready")
        attlo_ready = sem("attlo_ready")
        s1a_done = sem("s1a_done")
        s1a_ready = sem("s1a_ready")
        s1_turned = sem("s1_turned")
        nmax1_ready = sem("nmax1_ready")
        e1_ready = sem("e1_ready")
        p1_ready = sem("p1_ready")
        p1_turned = sem("p1_turned")
        p1Thi_ready = sem("p1Thi_ready")
        p1Tlo_ready = sem("p1Tlo_ready")
        out_done = sem("out_done")
        out_ready = sem("out_ready")

        def at(t, per, c):
            return t * per + c

        JCTX = 0
        JWK = JCTX + 2
        JV = JWK + KT
        JK = JV + 1
        JWQ = JK + KT
        JWQ1 = JWQ + KT
        JK1 = JWQ1 + KT
        JM = JK1 + KT
        JV1 = JM + KT
        JP = JV1 + KT
        JWO = JP + 1
        JVWT = JWO + KT
        JVW = JVWT + KT
        JW2 = JVW + B
        JCOL = JW2 + KT
        JC = JCOL + 1
        JWV = JC + 1
        NJ = JWV + KT
        assert JV % 2 == 0
        ACT_JOBS = (NJ + 1) // 2
        NCONST = 8 + KT + 2 * B
        SCORE_BANKS = [(0, 1, 7)[h % 3] for h in range(H - HPT)] + [0, 1] * (HPT // 2)
        TURN_BANKS = (7, 7, 0, 1)
        MAX_BANKS = (2, 7, 0, 1)
        V_BQ, V_BK, V_GAMMA, V_BETA, V_BOUT, V_BQ1, V_BK1, V_BV1, V_BV = range(NV)

        def taken(eng, n):
            if n % 2 == 0:
                eng.wait_ge(act_took, n // 2 + 1)
            else:
                eng.wait_ge(dve_took, n // 2 + 1)

        def vcol(v, k):
            return vcols[:, v * KT + k:v * KT + k + 1]

        block = ctx.enter_context(nc.Block())

        @block.sync
        def _(sp):
            w_in_v = w_in.rearrange("(t p) d -> p t d", p=P)

            def rows(dst, src, signal):
                sp.dma_start(dst[:, :, :], src.rearrange("(t p) d -> p t d", p=P)).then_inc(signal, 16)

            sp.dma_start(ctx_sb[:, :, :], ctx_in.rearrange("b j d -> j b d")).then_inc(s_ctx, 16)
            sp.dma_start(w_in_sb[:, KT:2 * KT, :], w_in_v[:, KT:2 * KT, :]).then_inc(s_wk, 16)
            vecs = [b_in[0:D], b_in[D:2 * D], gamma, beta, b_out, bq1, bk1, bv1, b_in[2 * D:3 * D]]
            for n, v in enumerate(vecs):
                sp.dma_start(vrows[n * KT:(n + 1) * KT, :], v.rearrange("(k p) -> k p", p=P)).then_inc(s_vec, 16)
            sp.dma_start(cb_i[:, :], char_bounds.rearrange("(c p) -> c p", p=P)).then_inc(s_vec, 16)
            sp.dma_start(w_in_sb[:, 0:KT, :], w_in_v[:, 0:KT, :]).then_inc(s_wq, 16)
            sp.dma_start(beta_rows[:, :], beta.rearrange("(o d) -> o d", o=1).broadcast_to([P, D])).then_inc(s_wq, 16)
            rows(wq1_sb, wq1, s_w1[0])
            wb = word_bounds.rearrange("(w o) -> w o", o=1)
            with nc.allow_non_contiguous_dma(reason="65 word boundaries, one per partition"):
                for dst, src in (((0, W, 0), (0, W)), ((0, W, 1), (1, W + 1)),
                                 ((0, 1, 2), (0, 1)), ((1, W, 2), (0, W - 1)),
                                 ((0, W - 1, 3), (2, W + 1)), ((W - 1, W, 3), (W, W + 1))):
                    sp.dma_start(wcol_i[dst[0]:dst[1], dst[2]:dst[2] + 1], wb[src[0]:src[1], :]).then_inc(s_word, 16)
            sp.dma_start(wb_i[:, :], word_bounds.rearrange("(o w) -> o w", o=1).broadcast_to([P, W + 1])).then_inc(s_word, 16)
            sp.wait_ge(job_done, JWK + KT)
            rows(wk1_sb, wk1, s_w1[1])
            for sub in range(SUB):
                sp.dma_start(xs[0][:, sub, :], x_t[0, 0, :, sub]).then_inc(x_loaded[0][sub], 16)
            rows(wv1_sb, wv1, s_w1[2])
            rows(w_out_sb, w_out, s_w1[3])
            sp.wait_ge(job_done, JWQ + KT)
            sp.wait_ge(qb_product, KT)
            rows(wo1_sb, wo1, s_w1[4])
            sp.dma_start(w_in_sb[:, 2 * KT:3 * KT, :], w_in_v[:, 2 * KT:3 * KT, :]).then_inc(s_wv, 16)
            sp.wait_ge(k_split, 1)
            for slot, src in enumerate((kT_hi, kT_hi, kT_lo)):
                for a in range(HPT):
                    for b in range(B):
                        sp.dma_start(kstack[DH * slot:DH * (slot + 1), b, a::HPT, :].bitcast(F32),
                                     src[DH * a:DH * (a + 1), :, b, :].bitcast(F32)).then_inc(s_kstack, 16)
            sp.wait_ge(job_done, JM + KT)
            for b in range(B):
                sp.dma_start(vw1[J:J + 1, b, :], bo1.rearrange("(o d) -> o d", o=1)).then_inc(s_bias1, 16)
                sp.dma_start(vw1[J + 1:J + 2, b, :], b_out.rearrange("(o d) -> o d", o=1)).then_inc(s_bias1, 16)
            for sub in range(SUB):
                sp.dma_start(xs[1][:, sub, :], x_t[1, 0, :, sub]).then_inc(x_loaded[1][sub], 16)

            def load(t_prev, q, s):
                for sub in range(SUB):
                    sp.wait_ge(x_stored[sub], at(t_prev, 16, 16))
                    sp.dma_start(xs[s][:, sub, :], x_t[s, q, :, sub]).then_inc(x_loaded[s][sub], 16)

            def stack(t, halves=1):
                ks = KT // halves
                for k0 in range(0, KT, ks):
                    sp.wait_ge(qlo_ready, at(t, KT, k0 + ks))
                    sp.wait_ge(qhi_ready, at(t, KT, k0 + ks))
                    for slot, src in enumerate((q_hi, q_lo, q_hi)):
                        for a in range(HPT):
                            sp.dma_start(qstack[DH * slot:DH * (slot + 1), a + k0 * HPT:(k0 + ks) * HPT:HPT, :].bitcast(F32),
                                         src[DH * a:DH * (a + 1), k0:k0 + ks, :].bitcast(F32))\
                              .then_inc(stack_loaded, 16)

            def spread_max(t):
                sp.wait_ge(mrows_ready, at(t, 1, 1))
                for i in range(2):
                    sp.dma_start(qstack[96:P, i * H // 2:(i + 1) * H // 2, :].bitcast(F32),
                                 mrows[:, :].unsqueeze(1).broadcast_to([2 * H, H // 2, T])).then_inc(mrows_spread[i], 16)

            def store(t, q, s):
                for sub in range(SUB):
                    sp.wait_ge(out_ready, at(t, SUB, SUB + sub + 1))
                    sp.dma_start(out_t[s, q, :, sub], xs[s][:, sub, :]).then_inc(x_stored[sub], 16)

            stack(0, halves=2)
            spread_max(0)

            def tile(t, q, s, more=True, loads=True):
                if more:
                    stack(t + 1)
                    spread_max(t + 1)
                store(t, q, s)
                if loads:
                    load(t, q + 1, s)

            with sp.Fori(0, QT - 1) as i:
                for s in range(2):
                    tile(2 * i + s, i, s)
            for s in range(2):
                tile(NT - 2 + s, QT - 1, s, more=s == 0, loads=False)
            for sub in range(SUB):
                sp.wait_ge(x_stored[sub], 16 * NT)

        @block.gpsimd
        def _(pool):
            n = 0

            def link(ins):
                nonlocal n
                n += 1
                ins.then_inc(pool_step, 1)
                pool.wait_ge(pool_step, n)

            consts = 0

            def ready(ins):
                nonlocal consts
                consts += 1
                ins.then_inc(const_ready, 1)
                pool.wait_ge(const_ready, consts)

            link(pool.memset(ident[:, :], 0.0))
            ready(pool.affine_select(out=ident[:, :], in_=ident[:, :], compare_op=ALU.not_equal, fill=1.0, base=0,
                                     pattern=[[-1, P]], channel_multiplier=1))
            ready(pool.memset(ones[:, :], 1.0))
            ready(pool.memset(kdiag_lo[:, :, :, :].bitcast(F32), 0.0))
            ready(pool.memset(kdiag_hi[:, :, :, :].bitcast(F32), 0.0))
            ready(pool.iota(tok[:, :], pattern=[[1, T]], base=0, channel_multiplier=0,
                      allow_small_or_imprecise_dtypes=True))
            ready(pool.iota(kcol[:, :], pattern=[[P, CC]], base=0, channel_multiplier=1,
                      allow_small_or_imprecise_dtypes=True))
            pool.memset(mhalf[:, :], -0.5).then_inc(pads_ready, 1)
            pool.wait_ge(pads_ready, 1)
            ready(pool.memset(maskw[64:P, :].bitcast(F32), 0.0))
            link(pool.memset(densel[:, :, :], 0.0))
            for g in range(KT):
                ready(pool.memset(densel[:, g, g::KT], 1.0))
            ready(pool.memset(densel[:, KT, :], 1.0))
            link(pool.memset(kstack[96:P, :, :, :].bitcast(F32), 0.0))
            for b in range(B):
                part = kstack[96:P, b, :, :]
                for base in (0, -H):
                    ins = pool.affine_select(out=part, in_=part.bitcast(F32), compare_op=ALU.not_equal, fill=-1.0, base=base,
                                             pattern=[[-1, H], [0, J]], channel_multiplier=1)
                    ready(ins)

            def root(t):
                pool.wait_ge(veps_ready, at(t, 1, 1))
                pool.tensor_tensor(rstd[:, :], veps[:, :], mhalf[:, :], ALU.pow).then_inc(rstd_ready, 1)

            root(0)
            pool.wait_ge(zhi_ready, 1)
            pool.memset(onehot[64:P, :].bitcast(F32), 0.0).then_inc(pads_ready, 1)
            pool.wait_ge(pads_ready, 2)
            with pool.Fori(0, NT - 1) as t:
                root(t + 1)
                for g in range(KT - 1):
                    pool.wait_ge(atthi_ready, at(t, KT, g + 1))
                    pool.tensor_tensor(attT_lo[:, g, :], att[:, g % 2, :], attT_hi[:, g, :],
                                       ALU.subtract).then_inc(attlo_ready, 1)

        @block.tensor
        def _(pe):
            def job(n):
                if n >= 8:
                    taken(pe, n - 8)
                return bank[n % 8]

            def turn_weight(n0, src, row0, k):
                b = job(n0 + k)
                for e in range(KT):
                    last = pe.transpose(b[:, e * P:(e + 1) * P], src[:, row0 + e, k * P:(k + 1) * P], ident[:, :])
                last.then_inc(job_done, 1)

            def product(n, terms, shape):
                b = job(n)
                for i, (l, r) in enumerate(terms):
                    last = pe.matmul(b[0:shape[0], 0:shape[1]], l, r, start=i == 0, stop=i == len(terms) - 1)
                last.then_inc(job_done, 1)

            def mf(k):
                return m_f[:, k, :, :].rearrange("p b j -> p (b j)")

            pe.wait_ge(const_ready, 1)
            pe.wait_ge(s_ctx, 16)
            for n in range(2):
                b = job(JCTX + n)
                for kk in range(2):
                    for bb in range(B):
                        k = 2 * n + kk
                        last = pe.transpose(b[:, kk * BJ + bb * J:kk * BJ + (bb + 1) * J],
                                            ctx_sb[:, bb, k * P:(k + 1) * P], ident[0:J, 0:J])
                last.then_inc(job_done, 1)
            pe.wait_ge(s_wk, 16)
            for k in range(KT):
                turn_weight(JWK, w_in_sb, KT, k)
            pe.wait_ge(s_vec, 16 * (NV + 1))
            b = job(JV)
            pe.wait_ge(cb_ready, 1)
            pe.transpose(b[:, 0:NV * KT], vrows[:, :], ident[0:NV * KT, 0:NV * KT])
            pe.transpose(b[:, NV * KT:NV * KT + CC], cb_f[:, :], ident[0:CC, 0:CC]).then_inc(job_done, 1)
            for n in (JWK + 3, JWK + 2, JCTX, JCTX + 1):
                taken(pe, n)
            for m in range(KT):
                product(JK + m, [(wT1[:, k, m * P:(m + 1) * P], ctxT0[:, k, :]) for k in range(KT)], (P, BJ))
            pe.wait_ge(s_wq, 32)
            for k in range(KT):
                turn_weight(JWQ, w_in_sb, 0, k)
            pe.wait_ge(s_w1[0], 16)
            for k in range(KT):
                turn_weight(JWQ1, wq1_sb, 0, k)
            pe.wait_ge(s_w1[1], 16)
            for m in range(KT):
                product(JK1 + m, [(wk1_sb[:, k, m * P:(m + 1) * P], ctxT0[:, k, :]) for k in range(KT)], (P, BJ))
            taken(pe, JV)
            taken(pe, JK1 + 3)
            taken(pe, JK1 + 2)
            for m in range(KT):
                product(JM + m, [(wT1[:, k, m * P:(m + 1) * P], k1T[:, k, :]) for k in range(KT)], (P, BJ))
            pe.wait_ge(s_w1[2], 16)
            for m in range(KT):
                product(JV1 + m, [(wv1_sb[:, k, m * P:(m + 1) * P], ctxT0[:, k, :]) for k in range(KT)], (P, BJ))
            pe.wait_ge(pick_ready, CC)
            b = job(JP)
            for c in range(CC):
                last = pe.matmul(b[:, 0:1], pick[:, c, :], cb_c[:, c:c + 1], start=c == 0, stop=c == CC - 1)
            last.then_inc(job_done, 1)
            pe.wait_ge(s_w1[3], 16)
            for k in range(KT):
                turn_weight(JWO, w_out_sb, 0, k)
            taken(pe, JV1 + 3)
            taken(pe, JV1 + 2)
            pe.wait_ge(s_w1[4], 16)
            for m in range(KT):
                product(JVWT + m, [(wo1_sb[:, k, m * P:(m + 1) * P], v1T[:, k, :]) for k in range(KT)], (P, BJ))
            for m in range(KT):
                taken(pe, JVWT + m)
            for bb in range(B):
                b = job(JVW + bb)
                for k in range(KT):
                    last = pe.transpose(b[0:J, k * P:(k + 1) * P], vwT[:, k, bb * J:(bb + 1) * J], ident[:, :])
                last.then_inc(job_done, 1)
            taken(pe, JM + 3)
            taken(pe, JM + 2)
            for m in range(KT):
                product(JW2 + m, [(w_out_sb[:, k, m * P:(m + 1) * P], mf(k)) for k in range(KT)], (P, BJ))
            pe.wait_ge(const_ready, 2)
            product(JCOL, [(ones[:, :], mf(k)) for k in range(KT)], (P, BJ))
            pe.wait_ge(bq1_ready, 1)
            b = job(JC)
            for bb in range(B):
                for k in range(KT):
                    pe.matmul(b[0:J, bb:bb + 1], m_f[:, k, bb, :], vcol(V_BOUT, k), start=k == 0, stop=False)
                for k in range(KT):
                    last = pe.matmul(b[0:J, bb:bb + 1], k1T[:, k, bb * J:(bb + 1) * J], bq1_cols[:, k:k + 1],
                                     start=False, stop=k == KT - 1)
            last.then_inc(job_done, 1)
            pe.wait_ge(s_wv, 16)
            for k in range(KT):
                turn_weight(JWV, w_in_sb, 2 * KT, k)

            def turn_z(t, sub, z_part=None):
                pe.wait_ge(z_ready, at(t, SUB, sub + 1))
                if sub == 1:
                    pe.wait_ge(zhi_ready, at(t, SUB, sub))
                    pe.wait_ge(zlo_ready, at(t, SUB, sub))
                b = bank[TURN_BANKS[sub]]
                src = z[:, sub] if z_part is None else z_part
                for k in range(KT):
                    last = pe.transpose(b[:, k * P:(k + 1) * P], src[:, k * P:(k + 1) * P], ident[:, :])
                last.then_inc(z_turned, 1)

            def split3(o, lhs, rhs, ks):
                n, total = 0, 3 * len(ks)
                for k in ks:
                    for l, r in ((0, 0), (0, 1), (1, 0)):
                        last = pe.matmul(o, lhs(l, k), rhs(r, k), start=n == 0, stop=n == total - 1)
                        n += 1
                return last

            wq = (wqT_hi, wqT_lo)
            wo = (woT_hi, woT_lo)
            zt = (zT_hi, zT_lo)
            aT = (attT_hi, attT_lo)
            qh = (q_hi, q_lo)
            kd = (kdiag_hi, kdiag_lo)
            mm = (m_hi, m_lo)
            w2 = (w2_hi, w2_lo)

            def project_q(t, s, t_prev=None):
                pe.wait_ge(zlo_ready, at(t, SUB, SUB))
                pe.wait_ge(zhi_ready, at(t, SUB, SUB))
                for m in range(KT):
                    if m == 2 and t_prev is not None:
                        pe.wait_ge(rd_ready, at(t_prev, 1, 1))
                    if m == 3:
                        pe.wait_ge(qlo_ready, at(t, KT, 1))
                        pe.wait_ge(qhi_ready, at(t, KT, 1))
                    split3(bank[m % 3][:, :], lambda l, k: wq[l][:, k, m * P:(m + 1) * P],
                           lambda r, k: zt[r][:, k, :], range(KT)).then_inc(q_done, 1)
                pe.wait_ge(qlo_ready, at(t, KT, 2))
                pe.wait_ge(qhi_ready, at(t, KT, 2))
                split3(bank[1][0:J, :], lambda l, k: mm[l][:, k, s, :],
                       lambda r, k: zt[r][:, k, :], range(KT)).then_inc(s1z_done, 1)

            def max_scores(t, s):
                for sub in range(SUB):
                    for g in range(KT):
                        u = sub * KT + g
                        if u < KT:
                            pe.wait_ge(qlo_ready, at(t, KT, 3 if u < 2 else 4))
                            pe.wait_ge(qhi_ready, at(t, KT, 3 if u < 2 else 4))
                            if u == 3:
                                pe.wait_ge(s1z_ready, at(t, 1, 1))
                        else:
                            pe.wait_ge(max_taken, at(t, SUB * KT, u - KT + 1))
                        split3(bank[MAX_BANKS[u % KT]][:, 0:GJ], lambda l, k: qh[l][:, g, sub * P:(sub + 1) * P],
                               lambda r, k: kd[r][:, s, g, :], [0]).then_inc(maxs_done, 1)

            def turn_max(t):
                pe.wait_ge(mx_ready, at(t, 1, 1))
                for sub in range(SUB):
                    last = pe.transpose(bank[1][0:2 * H, sub * P:(sub + 1) * P], mx2[:, sub, :], ident[:, :])
                last.then_inc(mx_turned, 1)

            def scores(t, q, s, h):
                if h == 0:
                    pe.wait_ge(mrows_spread[0], at(t, 16, 16))
                    pe.wait_ge(onehot_ready, at(q, 1, 1))
                    pe.wait_ge(stack_loaded, at(t + 1, 16 * 3 * HPT, 16 * 3 * HPT))
                if h == NPROB - 2:
                    pe.wait_ge(mrows_spread[1], at(t, 16, 16))
                before = [e for e in range(h) if SCORE_BANKS[e] == SCORE_BANKS[h]]
                if before:
                    pe.wait_ge(prob_ready, at(t, H, before[-1] + 1))
                b = bank[SCORE_BANKS[h]][0:J, :]
                pe.matmul(b, kstack[:, s, h, :], qstack[:, h, :], start=True, stop=False)
                pe.matmul(b, maskw[:, :], onehot[:, :], start=False, stop=True).then_inc(scores_done, 1)

            def attend(t, s, g, last_tile=False):
                pe.wait_ge(prob_ready, at(t, H, (g + 1) * HPT))
                pe.wait_ge(out_ready, at(t, SUB, g + 1))
                for a in range(HPT):
                    h = g * HPT + a
                    pe.matmul(bank[3 + g][a * DH:(a + 1) * DH, :], v0[:, s, h * DH:(h + 1) * DH],
                              prob[:, h % NPROB, :], start=True, stop=True)
                if last_tile and g:
                    pe.wait_ge(rd_ready, at(t, 1, g))
                for a in range(HPT):
                    h = g * HPT + a
                    last = pe.matmul(bank[2][a * DH:(a + 1) * DH, :], densel[:, KT if last_tile else g, :],
                                     prob[:, h % NPROB, :], start=last_tile or g == 0, stop=last_tile or g == KT - 1)
                last.then_inc(group_used, 1)

            def second_scores(t, s):
                pe.wait_ge(max_taken, at(t + 1, SUB * KT, SUB * KT - 3))
                pe.wait_ge(attlo_ready, at(t, KT, KT))
                pe.wait_ge(atthi_ready, at(t, KT, KT))
                split3(bank[2][0:J, :], lambda l, k: w2[l][:, k, s, :],
                       lambda r, k: aT[r][:, k, :], range(KT)).then_inc(s1a_done, 1)

            def turn_second(t, s, more):
                if more:
                    pe.wait_ge(max_taken, at(t + 1, SUB * KT, SUB * KT - 1))
                pe.wait_ge(s1z_ready, at(t, 1, 1))
                pe.wait_ge(s1a_ready, at(t, 1, 1))
                for sub in range(SUB):
                    pe.transpose(bank[7][:, sub * J:(sub + 1) * J], s1z[:, s, sub * P:(sub + 1) * P], ident[0:J, 0:J])
                for sub in range(SUB):
                    last = pe.transpose(bank[0][:, sub * J:(sub + 1) * J], s1t[0:J, sub * P:(sub + 1) * P],
                                        ident[0:J, 0:J])
                last.then_inc(s1_turned, 1)

            def second_part(t, s, k):
                pe.wait_ge(attlo_ready, at(t, KT, k + 1))
                pe.wait_ge(atthi_ready, at(t, KT, k + 1))
                for l, r in ((0, 0), (0, 1), (1, 0)):
                    last = pe.matmul(bank[7][0:J, :], w2[l][:, k, s, :], aT[r][:, k, :],
                                     start=k == 0 and l + r == 0, stop=k == KT - 1 and l == 1)
                if k == KT - 1:
                    last.then_inc(s1a_done, 1)

            def out_part(t, sub, ks):
                for k in ks:
                    for l, r in ((0, 0), (0, 1), (1, 0)):
                        pe.matmul(bank[3 + sub][:, :], aT[l][:, k, sub * P:(sub + 1) * P], wo[r][:, k, :],
                                  start=k == 0 and l + r == 0, stop=False)

            def out_proj(t, sub):
                out_part(t, sub, range(KT))

            def turn_p1(t):
                pe.wait_ge(p1_ready, at(t, 1, 1))
                for sub in range(SUB):
                    last = pe.transpose(bank[7][0:J + 2, sub * P:(sub + 1) * P], p1[:, sub, :], ident[:, :])
                last.then_inc(p1_turned, 1)

            def second_out(t, s, sub):
                pe.wait_ge(p1Thi_ready, at(t, 1, 1))
                pe.wait_ge(p1Tlo_ready, at(t, 1, 1))
                part = slice(sub * P, (sub + 1) * P)
                pe.matmul(bank[3 + sub][:, :], p1T_hi[:, part], vw1_hi[:, s, :], start=False, stop=False)
                pe.matmul(bank[3 + sub][:, :], p1T_hi[:, part], vw1_lo[:, s, :], start=False, stop=False)
                pe.matmul(bank[3 + sub][:, :], p1T_lo[:, part], vw1_hi[:, s, :],
                          start=False, stop=True).then_inc(out_done, 1)

            def v0_transposed(m):
                for k in range(KT):
                    last = pe.matmul(bank[3 + m][:, 0:BJ], wT0[:, k, m * P:(m + 1) * P], ctxT0[:, k, :],
                                     start=k == 0, stop=k == KT - 1)
                last.then_inc(v0T_done, 1)

            taken(pe, NJ - 1 - (NJ - 1 - 7) % 8)
            turn_z(0, 0, att[:, 0])
            for n in range(NJ - 8, NJ):
                taken(pe, n)
            v0_transposed(0)
            turn_z(0, 1, att[:, 1])
            turn_z(0, 2, att[:, 0])
            turn_z(0, 3, att[:, 1])
            v0_transposed(1)
            pe.wait_ge(act_prepared, 1)
            pe.wait_ge(dve_prepared, 1)
            project_q(0, 0)
            max_scores(0, 0)
            v0_transposed(2)
            turn_max(0)
            v0_transposed(3)
            pe.wait_ge(v0T_ready, KT)
            for bb in range(B):
                for k in range(KT):
                    last = pe.transpose(bank[3 + bb][0:J, k * P:(k + 1) * P], v0T[:, k, bb * J:(bb + 1) * J],
                                        ident[:, :])
                last.then_inc(v0_done, 1)
            pe.wait_ge(v0_ready, B)
            pe.wait_ge(const_ready, NCONST)
            pe.wait_ge(pads_ready, 2)

            def tile(t, q, s, more=True):
                n, ns = t + 1, 1 - s
                for h in range(AHEAD):
                    scores(t, q, s, h)
                for g in range(KT):
                    for h in range(g * HPT + AHEAD, min((g + 1) * HPT + AHEAD, H)):
                        scores(t, q, s, h)
                    if more and g == KT - 2:
                        pe.wait_ge(prob_ready, at(t, H, (g + 1) * HPT))
                        turn_z(n, 0)
                    if more and g == KT - 1:
                        turn_z(n, 1)
                        pe.wait_ge(prob_ready, at(t, H, H - 1))
                        turn_z(n, 2)
                        pe.wait_ge(prob_ready, at(t, H, H))
                        turn_z(n, 3)
                    if not more and g == KT - 1:
                        second_part(t, s, 0)
                    attend(t, s, g, last_tile=not more)
                if more:
                    project_q(n, ns, t)
                    max_scores(n, ns)
                    second_scores(t, s)
                    turn_max(n)
                    out_proj(t, 0)
                    turn_second(t, s, more)
                    out_proj(t, 1)
                    out_proj(t, 2)
                    turn_p1(t)
                    out_part(t, 3, range(KT - 1))
                else:
                    second_part(t, s, 1)
                    second_part(t, s, 2)
                    for sub in range(2):
                        out_part(t, sub, range(KT - 1))
                    second_part(t, s, 3)
                    for sub in range(2):
                        out_part(t, sub, (KT - 1,))
                    turn_second(t, s, more)
                    out_proj(t, 2)
                    out_part(t, 3, (0,))
                    turn_p1(t)
                    out_part(t, 3, range(1, KT))
                    for sub in range(SUB):
                        second_out(t, s, sub)
                    return
                for sub in range(SUB - 1):
                    second_out(t, s, sub)
                out_part(t, 3, (KT - 1,))
                second_out(t, s, 3)

            with pe.Fori(0, QT - 1) as i:
                for s in range(2):
                    tile(2 * i + s, i, s)
            tile(NT - 2, QT - 1, 0)
            tile(NT - 1, QT - 1, 1, more=False)

        def takes(n):
            b = bank[n % 8]
            for j0, dst in ((JWQ, wT0), (JWK, wT1), (JWV, wT0), (JWO, wT0), (JWQ1, wT1)):
                if j0 <= n < j0 + KT:
                    return dst[:, n - j0, :], b[:, :], None, None
            if JCTX <= n < JCTX + 2:
                k = 2 * (n - JCTX)
                return ctxT0[:, k:k + 2, :].rearrange("p k j -> p (k j)"), b[:, 0:2 * BJ], None, None
            if JVW <= n < JVW + B:
                return vw1[0:J, n - JVW, :], b[0:J, :], None, None
            for j0, dst, v, f in ((JK, kT, V_BK, None), (JK1, k1T, V_BK1, None), (JV1, v1T, V_BV1, None),
                                  (JM, m_f, None, SCALE1), (JW2, w2_f, None, None), (JVWT, vwT, None, None)):
                if j0 <= n < j0 + KT:
                    d = dst[:, n - j0]
                    if len(d.shape) == 3:
                        d = d.rearrange("p b j -> p (b j)")
                    return d, b[:, 0:BJ], None if v is None else vcol(v, n - j0), f
            if n == JCOL:
                return colm[:, :, :].rearrange("p b j -> p (b j)"), b[:, 0:BJ], None, None
            if n == JC:
                return c_col[:, :], b[0:J, 0:B], None, None
            if n == JP:
                return ce_cs[:, :], b[:, 0:1], None, None

        @block.scalar
        def _(act):
            def take(n):
                act.wait_ge(job_done, n + 1)
                if n == JV:
                    b = bank[JV % 8]
                    act.activation(cb_c[:, :], b[:, NV * KT:NV * KT + CC], ACT.Copy).then_inc(cb_ready, 1)
                    act.activation(vcols[:, :], b[:, 0:NV * KT], ACT.Copy).then_inc(act_took, 1)
                    return
                dst, src, bias, factor = takes(n)
                if bias is not None:
                    taken(act, JV)
                    act.activation(dst, src, ACT.Identity, bias=bias).then_inc(act_took, 1)
                else:
                    act.activation(dst, src, ACT.Copy, scale=1.0 if factor is None else factor)\
                       .then_inc(act_took, 1)

            def take_all(j0, j1):
                for n in range(j0 + j0 % 2, j1, 2):
                    take(n)

            take_all(JCTX, JWQ)
            for n in range(JK, JK + KT):
                taken(act, n)
            act.activation(kT_hi[:, :, :, :], kT[:, :, :, :], ACT.Copy).then_inc(hi_done, 1)
            take_all(JWQ, JWQ1)
            act.wait_ge(gs_ready, 1)
            for k in range(KT):
                taken(act, JWQ + k)
                act.activation(wqT_hi[:, k, :], wT0[:, k, :], ACT.Copy, scale=gs[:, k:k + 1]).then_inc(hi_done, 1)
            take_all(JWQ1, JK1)
            take_all(JK1, JV1)
            for n in range(JM, JM + KT):
                taken(act, n)
            act.activation(m_hi[:, :, :, :], m_f[:, :, :, :], ACT.Copy).then_inc(hi_done, 1)
            take_all(JV1, JWO)
            act.wait_ge(const_ready, 4)
            act.wait_ge(hi_done, 1)
            for b in range(B):
                for a in range(HPT):
                    rows = slice(DH * a, DH * (a + 1))
                    act.activation(kdiag_hi[rows, b, :, a * J:(a + 1) * J], kT_hi[rows, :, b, :], ACT.Copy)\
                       .then_inc(kdiag_done, 1)
            act.wait_ge(wq_split, KT)
            take_all(JWO, JVWT)
            act.wait_ge(k_split, 1)
            take_all(JVWT, JVW)
            for k in range(KT):
                taken(act, JWO + k)
                act.activation(woT_hi[:, k, :], wT0[:, k, :], ACT.Copy).then_inc(hi_done, 1)
            take_all(JVW, JW2)
            taken(act, JVW)
            taken(act, JVW + 1)
            act.wait_ge(s_bias1, 16 * 2 * B)
            act.activation(vw1_hi[:, :, :], vw1, ACT.Copy).then_inc(hi_done, 1)
            take_all(JW2, JCOL)
            for n in range(JW2, JW2 + KT):
                taken(act, n)
            act.activation(w2_hi[:, :, :, :], w2_f[:, :, :, :], ACT.Copy).then_inc(hi_done, 1)
            take_all(JCOL, JWV)
            act.wait_ge(wo_split, KT)
            take_all(JWV, NJ)
            act.wait_ge(act_took, ACT_JOBS)
            act.wait_ge(hi_done, 2 * KT + 4)
            act.activation(act_mark[:, :], vcols[:, 0:1], ACT.Copy).then_inc(act_prepared, 1)

            def z_high(t, sub):
                act.wait_ge(z_turned, at(t, SUB, sub + 1))
                act.activation(zT_hi[:, :, sub * P:(sub + 1) * P],
                               bank[TURN_BANKS[sub]][:, :].rearrange("p (k c) -> p k c", k=KT), ACT.Copy).then_inc(zhi_ready, 1)

            def q_high(t, s, before=None):
                for m in range(KT):
                    if before is not None and m >= 2:
                        att_high(before, m - 2)
                    act.wait_ge(q_done, at(t, KT, m + 1))
                    act.activation(q_hi[:, m, :], bank[m % 3][:, :], ACT.Identity,
                                   bias=q_bias[:, m:m + 1]).then_inc(qhi_ready, 1)
                act.wait_ge(s1z_done, at(t, 1, 1))
                act.activation(s1z[:, s, :], bank[1][0:J, :], ACT.Copy).then_inc(s1z_ready, 1)

            def max_rows(t):
                act.wait_ge(mx_turned, at(t, 1, 1))
                act.activation(mrows[:, :], bank[1][0:2 * H, :], ACT.Copy).then_inc(mrows_ready, 1)

            def att_high(t, g):
                act.wait_ge(att_ready, at(t, KT, g + 1))
                act.activation(attT_hi[:, g, :], att[:, g % 2, :], ACT.Copy).then_inc(atthi_ready, 1)

            act.wait_ge(s_kstack, 16 * 3 * HPT * B)
            act.wait_ge(dve_prepared, 1)
            for sub in range(SUB):
                z_high(0, sub)
            q_high(0, 0)
            max_rows(0)
            for m in range(0, KT, 2):
                act.wait_ge(v0T_done, m + 1)
                act.activation(v0T[:, m, :], bank[3 + m][:, 0:BJ], ACT.Identity, bias=bv_cols[:, m:m + 1])\
                   .then_inc(v0T_ready, 1)
            act.wait_ge(v0_done, 1)
            act.activation(v0[:, 0, :], bank[3][0:J, :], ACT.Copy).then_inc(v0_ready, 1)

            def tile(t, s, more=True):
                n, ns = t + 1, 1 - s
                for h in range(H):
                    act.wait_ge(scores_done, at(t, H, h + 1))
                    if h >= NPROB:
                        act.wait_ge(group_used, at(t, KT, (h - NPROB) // HPT + 1))
                    act.activation(prob[:, h % NPROB, :], bank[SCORE_BANKS[h]][0:J, :], ACT.Exp).then_inc(prob_ready, 1)
                    if more and h == H - 3:
                        z_high(n, 0)
                    if not more and h in (H - 7, H - 3):
                        att_high(t, (h - H + 7) // HPT)
                if not more:
                    att_high(t, 2)
                if more:
                    for sub in range(1, SUB):
                        z_high(n, sub)
                    q_high(n, ns, before=t)
                    att_high(t, 2)
                att_high(t, 3)
                act.wait_ge(s1a_done, at(t, 1, 1))
                act.activation(s1t[0:J, :], bank[2 if more else 7][0:J, :], ACT.Identity,
                               bias=c_col[:, s:s + 1]).then_inc(s1a_ready, 1)
                if more:
                    max_rows(n)
                act.wait_ge(nmax1_ready, at(t, 1, 1))
                for sub in range(SUB):
                    act.activation(e1[:, sub, :], p1[:, sub, 0:J], ACT.Exp, bias=nmax1[:, sub:sub + 1],
                                   accum_out=sum1[:, sub:sub + 1]).then_inc(e1_ready, 1)
                act.wait_ge(p1_turned, at(t, 1, 1))
                act.activation(p1T_hi[:, :], bank[7][0:J + 2, :], ACT.Copy).then_inc(p1Thi_ready, 1)

            with act.Fori(0, QT - 1) as i:
                for s in range(2):
                    tile(2 * i + s, s)
            tile(NT - 2, 0)
            tile(NT - 1, 1, more=False)

        @block.vector
        def _(dve):
            nprep = 0

            def link(ins):
                nonlocal nprep
                nprep += 1
                ins.then_inc(prep_step, 1)
                dve.wait_ge(prep_step, nprep)

            def take(n):
                dve.wait_ge(job_done, n + 1)
                dst, src, bias, factor = takes(n)
                if bias is not None:
                    dve.tensor_scalar(dst, src, bias, None, ALU.add).then_inc(dve_took, 1)
                elif factor is not None:
                    dve.tensor_scalar(dst, src, factor, None, ALU.mult).then_inc(dve_took, 1)
                else:
                    dve.tensor_copy(dst, src).then_inc(dve_took, 1)

            cnt = [0]
            base = [0]

            def count(ins):
                cnt[0] += 1
                ins.then_inc(step, 1)

            def own(ins):
                count(ins)
                dve.wait_ge(step, base[0] + cnt[0])

            def own_all(instructions):
                for ins in instructions[:-1]:
                    count(ins)
                own(instructions[-1])

            def normalise(t, q, s):
                for sub in range(SUB):
                    dve.wait_ge(x_loaded[s][sub], at(q, 16, 16))
                    ins = dve.bn_stats(stats[:, sub, :], xs[s][:, sub, :])
                    if sub < SUB - 1:
                        count(ins)
                own(ins)
                even, odd = stats[:, :, 0:3], stats[:, :, 3:6]
                count(dve.tensor_tensor(mean[s][:, :], even[:, :, 1], odd[:, :, 1], ALU.add))
                count(dve.tensor_tensor(mdiff[:, :], even[:, :, 1], odd[:, :, 1], ALU.subtract))
                own(dve.tensor_tensor(veps[:, :], even[:, :, 2], odd[:, :, 2], ALU.add))
                count(dve.tensor_scalar(mean[s][:, :], mean[s][:, :], 0.5, None, ALU.mult))
                count(dve.tensor_tensor(mdiff[:, :], mdiff[:, :], mdiff[:, :], ALU.mult))
                own(dve.tensor_scalar(veps[:, :], veps[:, :], 1.0 / D, EPS, ALU.mult, ALU.add))
                dve.scalar_tensor_tensor(out=veps[:, :], in0=mdiff[:, :], scalar=0.25, in1=veps[:, :],
                                         op0=ALU.mult, op1=ALU.add).then_inc(veps_ready, 1)
                dve.wait_ge(rstd_ready, at(t, 1, 1))
                own(dve.reciprocal(std[s][:, :], rstd[:, :]))

            def z_part(t, s, sub, dst=None):
                dve.tensor_scalar(z[:, sub, :] if dst is None else dst, xs[s][:, sub, :], mean[s][:, sub:sub + 1], rstd[:, sub:sub + 1],
                                  ALU.subtract, ALU.mult).then_inc(z_ready, 1)

            def z_low(t, sub):
                dve.wait_ge(zhi_ready, at(t, SUB, sub + 1))
                part = slice(sub * P, (sub + 1) * P)
                dve.tensor_tensor(zT_lo[:, :, part], bank[TURN_BANKS[sub]][:, :].rearrange("p (k c) -> p k c", k=KT),
                                  zT_hi[:, :, part], ALU.subtract).then_inc(zlo_ready, 1)

            def q_low(t, m):
                dve.wait_ge(qhi_ready, at(t, KT, m + 1))
                dve.scalar_tensor_tensor(out=q_lo[:, m, :], in0=bank[m % 3][:, :], scalar=q_bias[:, m:m + 1],
                                         in1=q_hi[:, m, :], op0=ALU.add, op1=ALU.subtract).then_inc(qlo_ready, 1)

            def take_max(t, us=range(SUB * KT)):
                for u in us:
                    sub, g = u // KT, u % KT
                    dve.wait_ge(maxs_done, at(t, SUB * KT, u + 1))
                    dve.tensor_reduce(mx[:, sub, g * HPT:(g + 1) * HPT],
                                      bank[MAX_BANKS[u % KT]][:, 0:GJ].rearrange("p (a j) -> p a j", a=HPT), AX.X,
                                      ALU.max).then_inc(max_taken, 1)

            def split_max(t):
                dve.wait_ge(max_taken, at(t, SUB * KT, SUB * KT))
                own(dve.tensor_copy(mx_hr, mx))
                own(dve.tensor_copy(mx2[:, :, 0:H], mx_hr))
                dve.tensor_tensor(mx2[:, :, H:2 * H], mx, mx_hr, ALU.subtract).then_inc(mx_ready, 1)

            def one_hot():
                own(dve.tensor_scalar(begun[:, :], tok[:, :], wlo[:, :], None, ALU.is_ge))
                dve.scalar_tensor_tensor(out=onehot[0:W, :], in0=tok[:, :], scalar=whi[:, :], in1=begun[:, :],
                                         op0=ALU.is_lt, op1=ALU.mult).then_inc(onehot_ready, 1)

            def invert(t):
                dve.wait_ge(group_used, at(t, KT, KT))
                dve.reciprocal(rd[:, :], bank[2][:, :]).then_inc(rd_ready, 1)

            def divide_last(t, g):
                if g == KT - 1:
                    att_low(t, g - 1)
                dve.wait_ge(group_used, at(t, KT, g + 1))
                dve.reciprocal(rd_last[:, g % 2, :], bank[2][:, :]).then_inc(rd_ready, 1)
                dve.wait_ge(rd_ready, at(t, 1, g + 1))
                if g >= 2:
                    dve.wait_ge(attlo_ready, at(t, KT, g - 1))
                dve.tensor_tensor(att[:, g % 2, :], bank[3 + g][:, :], rd_last[:, g % 2, :], ALU.mult).then_inc(att_ready, 1)
                if g in (1, 2):
                    att_low(t, g - 1)

            def divide(t, g):
                own(dve.stream_shuffle(att[:, g % 2, :], rd[:, :], [g] * DH))
                dve.tensor_tensor(att[:, g % 2, :], bank[3 + g][:, :], att[:, g % 2, :], ALU.mult).then_inc(att_ready, 1)

            def att_low(t, g):
                dve.wait_ge(atthi_ready, at(t, KT, g + 1))
                dve.tensor_tensor(attT_lo[:, g, :], att[:, g % 2, :], attT_hi[:, g, :],
                                  ALU.subtract).then_inc(attlo_ready, 1)

            def take_all(j0, j1):
                for n in range(j0 + 1 - j0 % 2, j1, 2):
                    take(n)

            def pick_chunks(c0, c1):
                for c in range(c0, c1):
                    dve.tensor_scalar(pick[:, c, :], widx[:, :], kcol[:, c:c + 1], None, ALU.is_equal)\
                       .then_inc(pick_ready, 1)

            take_all(JCTX, JV)
            dve.wait_ge(s_vec, 16 * (NV + 1))
            dve.tensor_scalar(cb_f[:, :], cb_i[:, :], 0, J, ALU.max, ALU.min).then_inc(cb_ready, 1)
            taken(dve, JV)
            dve.tensor_copy(bv_cols[:, :], vcols[:, V_BV * KT:(V_BV + 1) * KT]).then_inc(prep_lo, 1)
            dve.tensor_scalar(gs[:, :], vcols[:, V_GAMMA * KT:(V_GAMMA + 1) * KT], SCALE0, None,
                              ALU.mult).then_inc(gs_ready, 1)
            dve.wait_ge(s_wq, 32)
            for m in range(KT):
                dve.tensor_tensor(att[:, m % 2, :], w_in_sb[:, m, :], beta_rows[:, :], ALU.mult).then_inc(qb_product, 1)
                if m % 2:
                    take(JK + m - JK % 2)
                    dve.wait_ge(qb_product, m + 1)
                    dve.tensor_reduce(q_bias[:, m - 1:m + 1], att[:, :, :], AX.X, ALU.add).then_inc(qb_summed, 1)
                    dve.wait_ge(qb_summed, m // 2 + 1)
            link(dve.tensor_tensor(q_bias[:, :], q_bias[:, :], vcols[:, V_BQ * KT:(V_BQ + 1) * KT], ALU.add))
            link(dve.tensor_scalar(q_bias[:, :], q_bias[:, :], SCALE0, None, ALU.mult))
            dve.wait_ge(hi_done, 1)
            dve.tensor_tensor(kT_lo[:, :, :, :], kT[:, :, :, :], kT_hi[:, :, :, :], ALU.subtract).then_inc(k_split, 1)
            take_all(JWQ, JWQ1)
            take_all(JWQ1, JM)
            dve.wait_ge(gs_ready, 1)
            for k in range(KT):
                dve.wait_ge(hi_done, 2 + k)
                dve.scalar_tensor_tensor(out=wqT_lo[:, k, :], in0=wT0[:, k, :], scalar=gs[:, k:k + 1],
                                         in1=wqT_hi[:, k, :], op0=ALU.mult, op1=ALU.subtract).then_inc(wq_split, 1)
            dve.wait_ge(const_ready, 6)
            dve.wait_ge(s_word, 16 * 7)
            link(dve.tensor_copy(wb32[:, :], wb_i[:, :]))
            dve.tensor_copy(widx[:, 0:W], wb32[:, 0:W])
            link(dve.tensor_scalar(widx[:, W:2 * W], wb32[:, 1:W + 1], 1.0, None, ALU.subtract))
            link(dve.tensor_scalar(widx2[:, :], widx[:, :], 0.0, float(NCB), ALU.is_lt, ALU.mult))
            link(dve.tensor_tensor(widx2[:, :], widx2[:, :], widx[:, :], ALU.add))
            link(dve.tensor_scalar(widx[:, :], widx2[:, :], 0.0, float(NCB - 1), ALU.max, ALU.min))
            pick_chunks(0, CC)
            dve.tensor_scalar(bq1_cols[:, :], vcols[:, V_BQ1 * KT:(V_BQ1 + 1) * KT], SCALE1, None, ALU.mult)\
               .then_inc(bq1_ready, 1)
            take_all(JM, JV1)
            dve.wait_ge(hi_done, KT + 2)
            dve.tensor_tensor(m_lo[:, :, :, :], m_f[:, :, :, :], m_hi[:, :, :, :], ALU.subtract).then_inc(prep_lo, 1)
            take_all(JV1, JWO)
            normalise(0, 0, 0)
            z_part(0, 0, 0, att[:, 0, :])
            z_part(0, 0, 1, att[:, 1, :])
            take_all(JWO, JVW)
            for k in range(KT):
                dve.wait_ge(hi_done, KT + 3 + k)
                dve.tensor_tensor(woT_lo[:, k, :], wT0[:, k, :], woT_hi[:, k, :], ALU.subtract).then_inc(wo_split, 1)
            dve.wait_ge(const_ready, 4)
            dve.wait_ge(k_split, 1)
            for b in range(B):
                for a in range(HPT):
                    rows = slice(DH * a, DH * (a + 1))
                    dve.tensor_copy(kdiag_lo[rows, b, :, a * J:(a + 1) * J], kT_lo[rows, :, b, :])\
                       .then_inc(kdiag_done, 1)
            take_all(JVW, JW2)
            link(dve.tensor_copy(wcol[:, :], wcol_i[:, :]))
            taken(dve, JP)
            link(dve.tensor_copy(cend[:, :], ce_cs[W:2 * W, :]))
            link(dve.tensor_copy(wlo[:, :], wcol[:, 0:1]))
            link(dve.tensor_copy(whi[:, :], wcol[:, 1:2]))
            bounds = ((ce_cs[0:W, :], cend[:, :]), (wcol[:, 2:3], wcol[:, 0:1]), (wcol[:, 1:2], wcol[:, 3:4]))
            for r, (lo, hi) in enumerate(bounds):
                link(dve.tensor_scalar(ge[:, r, :], tok[:, 0:J], lo, None, ALU.is_ge))
                link(dve.scalar_tensor_tensor(out=rng[:, r, :], in0=tok[:, 0:J], scalar=hi, in1=ge[:, r, :],
                                              op0=ALU.is_lt, op1=ALU.mult))
            link(dve.tensor_tensor(rng[:, 0, :], rng[:, 0, :], rng[:, 1, :], ALU.max))
            link(dve.tensor_tensor(rng[:, 0, :], rng[:, 0, :], rng[:, 2, :], ALU.max))
            dve.tensor_copy(maskw[0:W, :], rng[:, 0, :]).then_inc(prep_lo, 1)
            dve.wait_ge(hi_done, 2 * KT + 3)
            dve.tensor_tensor(vw1_lo[:, :, :], vw1, vw1_hi[:, :, :], ALU.subtract).then_inc(prep_lo, 1)
            take_all(JW2, JCOL)
            dve.wait_ge(hi_done, 2 * KT + 4)
            dve.tensor_tensor(w2_lo[:, :, :, :], w2_f[:, :, :, :], w2_hi[:, :, :, :], ALU.subtract).then_inc(prep_lo, 1)
            take_all(JCOL, NJ)
            dve.wait_ge(prep_lo, 5)
            dve.wait_ge(kdiag_done, 2 * B * HPT)
            dve.wait_ge(wo_split, KT)
            dve.wait_ge(dve_took, NJ - ACT_JOBS)
            dve.memset(p1ones[:, :], 1.0).then_inc(out_ready, SUB)
            dve.wait_ge(out_ready, SUB)
            dve.tensor_copy(dve_mark[:, :], p1ones[:, 0:1]).then_inc(dve_prepared, 1)

            dve.wait_ge(z_turned, 1)
            z_part(0, 0, 2, att[:, 0, :])
            z_low(0, 0)
            dve.wait_ge(z_turned, 2)
            z_part(0, 0, 3, att[:, 1, :])
            z_low(0, 1)
            z_low(0, 2)
            z_low(0, 3)
            for m in range(KT):
                q_low(0, m)
            one_hot()
            take_max(0)
            split_max(0)
            for m in range(1, KT, 2):
                dve.wait_ge(v0T_done, m + 1)
                dve.tensor_scalar(v0T[:, m, :], bank[3 + m][:, 0:BJ], bv_cols[:, m:m + 1], None, ALU.add)\
                   .then_inc(v0T_ready, 1)
            dve.wait_ge(v0_done, 2)
            dve.tensor_copy(v0[:, 1, :], bank[4][0:J, :]).then_inc(v0_ready, 1)
            own(dve.memset(p1[:, :, J:J + 2], 1.0))
            first = cnt[0]
            NSTEP = 2 * (SUB + 6 + 1 + 2 * SUB + 1 + SUB + 2 + KT) + 3

            def tile(t, q, s, more=True):
                n, ns, nq = t + 1, 1 - s, q + s
                if more:
                    normalise(n, nq, ns)
                    for sub in range(SUB):
                        z_part(n, ns, sub)
                    for sub in range(SUB):
                        z_low(n, sub)
                    invert(t)
                for g in range(KT):
                    if not more:
                        divide_last(t, g)
                        if g == KT - 1:
                            att_low(t, g)
                        continue
                    if g == 0:
                        dve.wait_ge(rd_ready, at(t, 1, 1))
                    if g >= 2:
                        dve.wait_ge(attlo_ready, at(t, KT, g - 1))
                    q_low(n, g)
                    divide(t, g)
                if more:
                    take_max(n, range(KT))
                    att_low(t, KT - 1)
                    take_max(n, range(KT, SUB * KT))
                    split_max(n)
                    dve.wait_ge(mx_ready, at(n, 1, 1))
                    if s == 1:
                        own(dve.tensor_scalar(wlo[:, :], wlo[:, :], float(T), None, ALU.subtract))
                        own(dve.tensor_scalar(whi[:, :], whi[:, :], float(T), None, ALU.subtract))
                        one_hot()
                own_all([dve.tensor_scalar(sc1b[:, sub, :], colm[:, s, :], mean[s][:, sub:sub + 1], None, ALU.mult)
                         for sub in range(SUB)])
                dve.wait_ge(s1_turned, at(t, 1, 1))
                own_all([dve.scalar_tensor_tensor(out=sc1b[:, sub, :], in0=bank[7][:, sub * J:(sub + 1) * J],
                                                  scalar=std[s][:, sub:sub + 1], in1=sc1b[:, sub, :],
                                                  op0=ALU.mult, op1=ALU.add) for sub in range(SUB)])
                own(dve.tensor_tensor(sc1, sc1b[:, :, :],
                                      bank[0][:, 0:SUB * J].rearrange("p (s j) -> p s j", s=SUB), ALU.add))
                dve.tensor_reduce(nmax1[:, :], sc1, AX.X, ALU.max, negate=True).then_inc(nmax1_ready, 1)
                dve.wait_ge(e1_ready, at(t, SUB, SUB))
                own(dve.reciprocal(rsum1[:, :], sum1[:, :]))
                for sub in range(SUB):
                    ins = dve.tensor_scalar(p1[:, sub, 0:J], e1[:, sub, :], rsum1[:, sub:sub + 1], None, ALU.mult)
                    if sub < SUB - 1:
                        count(ins)
                    else:
                        ins.then_inc(p1_ready, 1)
                dve.wait_ge(p1Thi_ready, at(t, 1, 1))
                dve.tensor_tensor(p1T_lo[:, :], bank[7][0:J + 2, :], p1T_hi[:, :], ALU.subtract)\
                   .then_inc(p1Tlo_ready, 1)
                for sub in range(SUB):
                    dve.wait_ge(out_done, at(t, SUB, sub + 1))
                    dve.tensor_tensor(xs[s][:, sub, :], bank[3 + sub][:, :], xs[s][:, sub, :],
                                      ALU.add).then_inc(out_ready, 1)

            with dve.Fori(0, QT - 1) as i:
                base[0] = i * NSTEP + first
                cnt[0] = 0
                for s in range(2):
                    tile(2 * i + s, i, s)
                assert cnt[0] == NSTEP, cnt[0]
            base[0] = (QT - 1) * NSTEP + first
            cnt[0] = 0
            tile(NT - 2, QT - 1, 0)
            tile(NT - 1, QT - 1, 1, more=False)


_INS = ["x", "ctx_1024", "itok_S_0_4092", "L0_xattn_word_boundaries", "L0_xattn_ln_gamma", "L0_xattn_ln_beta",
        "L0_xattn_in_proj_w", "L0_xattn_in_proj_b", "L0_xattn_out_w", "L0_xattn_out_b",
        "L1_xattn_Wq", "L1_xattn_bq", "L1_xattn_Wk", "L1_xattn_bk", "L1_xattn_Wv", "L1_xattn_bv",
        "L1_xattn_Wo", "L1_xattn_bo"]


def kernel(**inputs):
    import numpy as _np
    import concourse.bacc as _bacc
    from concourse import mybir as _mybir
    from concourse.bass_utils import run_bass_kernel_spmd as _run

    nc = _bacc.Bacc("TRN2", target_bir_lowering=False, num_devices=1)
    arrays, args = {}, []
    for name in _INS:
        a = _np.ascontiguousarray(inputs[name])
        arrays[f"in_{name}_dram"] = a
        args.append(nc.dram_tensor(f"in_{name}_dram", a.shape, _mybir.dt.from_np(a.dtype), kind="ExternalInput").ap())
    shape = tuple(inputs["x"].shape)
    args.append(nc.dram_tensor("out_0_dram", shape, _mybir.dt.float32, kind="ExternalOutput").ap())
    two_cross_attentions(nc, *args)
    r = _run(nc, [arrays], core_ids=[0])
    return r.results[0]["out_0_dram"]
```
